# Optimizing a Trainium2 kernel written in Bass

```python
import numpy as np
import jax
import jax.numpy as jnp

def _softmax(x, axis=-1):
    return jax.nn.softmax(x, axis=axis)

def _gelu(x):
    return jax.nn.gelu(x, approximate=True)

def _silu(x):
    return jax.nn.silu(x)

def _sigmoid(x):
    return jax.nn.sigmoid(x)

def _layernorm(x, axis=-1, eps=1e-05):
    m = jnp.mean(x, axis=axis, keepdims=True)
    v = jnp.var(x, axis=axis, keepdims=True)
    return (x - m) / jnp.sqrt(v + eps)

def _scatter_add(tgt, idx, src, axis=0):
    return tgt.at[idx].add(src)

def _segment_sum(src, seg, n):
    return jax.ops.segment_sum(src, seg, n)
kernel_name = 'mk_adj_resnorm_d2_adj_r2_38c70a'

def setup_inputs(seed: int=0):
    np.random.seed(seed)
    _w = jnp.asarray

    def _rec_inputs():
        import jax
        import jax.numpy as jnp
        _gk = jax.random.key(seed)
        x = -0.0005207 + 1.001 * jax.random.normal(jax.random.fold_in(_gk, 1), (8192, 128), jnp.float32)
        _a = jax.random.bernoulli(jax.random.fold_in(_gk, 2), 0.00195312, (8192, 8192))
        _a = jnp.logical_or(_a, jnp.eye(8192, dtype=bool))
        _af = _a.astype(jnp.float32)
        _af = _af * jax.random.uniform(jax.random.fold_in(_gk, 3), (8192, 8192), jnp.float32, 0.05, 1)
        adj = _af
        return (x, adj)
    x, adj = _rec_inputs()

    def _L0_gnn_setup():
        import jax, jax.numpy as jnp
        import numpy as np
        N = 8192
        C = 128
        F = 128
        key = jax.random.key(seed)
        k1, k2, k3, k4 = jax.random.split(key, 4)
        X = jax.random.normal(k1, (N, C), dtype=jnp.float32)
        adj = jax.random.uniform(k2, (N, N), dtype=jnp.float32)
        W = jax.random.normal(k3, (C, F), dtype=jnp.float32) * 0.05
        b = jax.random.normal(k4, (F,), dtype=jnp.float32) * 0.05
        return {'X': X, 'adj': adj, 'W': W, 'b': b}
    _L0_gnn_all = _L0_gnn_setup()
    _L0_gnn_in = {k: v for k, v in _L0_gnn_all.items() if k in ('W', 'b')}
    del _L0_gnn_all

    def _L1_gnn_setup():
        import jax, jax.numpy as jnp
        import numpy as np
        EPS = 1e-06
        PN_SCALE = 1.0

        def pair_norm(x):
            x = x - jnp.mean(x, axis=0, keepdims=True)
            rownorm_mean = jnp.sqrt(jnp.mean(jnp.sum(x * x, axis=1) + EPS))
            return PN_SCALE * x / rownorm_mean
        key = jax.random.key(seed)
        k1, k2, k3, k4 = jax.random.split(key, 4)
        N, IN, OUT = (8192, 128, 128)
        x = jax.random.normal(k1, (N, IN), dtype=jnp.float32)
        adj = jax.random.uniform(k2, (N, N), dtype=jnp.float32)
        bound = float(np.sqrt(6.0 / (IN + OUT)))
        weight = jax.random.uniform(k3, (IN, OUT), dtype=jnp.float32, minval=-bound, maxval=bound)
        self_weight = jax.random.uniform(k4, (IN, OUT), dtype=jnp.float32, minval=-bound, maxval=bound)
        return {'x': x, 'adj': adj, 'weight': weight, 'self_weight': self_weight}
    _L1_gnn_all = _L1_gnn_setup()
    _L1_gnn_in = {k: v for k, v in _L1_gnn_all.items() if k in ('weight', 'self_weight')}
    del _L1_gnn_all
    return {'x': x, 'adj': adj, 'L0_gnn_W': _L0_gnn_in['W'], 'L0_gnn_b': _L0_gnn_in['b'], 'L1_gnn_weight': _L1_gnn_in['weight'], 'L1_gnn_self_weight': _L1_gnn_in['self_weight']}

def reference(x, adj, L0_gnn_W, L0_gnn_b, L1_gnn_weight, L1_gnn_self_weight):
    import jax
    import jax.numpy as jnp

    def _L0_gnn_ref(X, adj, W, b):
        import jax, jax.numpy as jnp
        import numpy as np
        N = 8192
        C = 128
        F = 128
        adj_hat = adj + jnp.eye(adj.shape[0], dtype=adj.dtype)
        d_inv_sqrt = 1.0 / jnp.sqrt(jnp.sum(adj_hat, axis=1))
        adj_norm = adj_hat * d_inv_sqrt[:, None] * d_inv_sqrt[None, :]
        out = adj_norm @ (X @ W) + b
        return jax.nn.relu(out)

    def _L1_gnn_ref(x, adj, weight, self_weight):
        import jax, jax.numpy as jnp
        import numpy as np
        EPS = 1e-06
        PN_SCALE = 1.0

        def pair_norm(x):
            x = x - jnp.mean(x, axis=0, keepdims=True)
            rownorm_mean = jnp.sqrt(jnp.mean(jnp.sum(x * x, axis=1) + EPS))
            return PN_SCALE * x / rownorm_mean
        support = x @ weight
        output = support + adj @ support
        output = output + x @ self_weight
        output = jax.nn.relu(output)
        return pair_norm(output)
    x = _layernorm(x + _L0_gnn_ref(x, adj, L0_gnn_W, L0_gnn_b), axis=-1)
    x = _layernorm(x + _L1_gnn_ref(x, adj, L1_gnn_weight, L1_gnn_self_weight), axis=-1)
    return x

_drawn_inputs = setup_inputs


def setup_inputs(seed=0):
    import zlib

    import numpy as np

    out = dict(_drawn_inputs(seed))
    spreads = {}
    factors = {}
    for name, (base, spread) in spreads.items():
        noise = np.random.default_rng([zlib.crc32(name.encode()), seed]).standard_normal(out[name].shape)
        drawn = base * np.exp(spread * noise) if base else spread * noise
        out[name] = jnp.asarray(drawn.astype(out[name].dtype))
    for name, factor in factors.items():
        out[name] = (out[name] * factor).astype(out[name].dtype)
    return out
```

```python
import concourse.bass as bass
from concourse import mybir
from contextlib import ExitStack


def graph_kernel(nc, x, xT, adjT, adjN, W0, b_rows, W1, Wself, out):
    f32 = mybir.dt.float32
    f32r = mybir.dt.float32r
    ACT = mybir.ActivationFunctionType
    ALU = mybir.AluOpType
    AX = mybir.AxisListType
    ds = bass.ds

    P = 128
    N = x.shape[0]
    F = x.shape[1]
    assert F == P
    BLK = 1024
    NB = N // BLK
    Q = 4
    JB = BLK // Q // P
    TILE = JB * BLK
    H = BLK // 512
    HALF = 512
    G = HALF // P
    EPS_LN = 1e-5
    EPS_PN = 1e-6
    assert NB >= 4 and JB == 2 and H == 2

    LOWER = NB * (NB - 1) // 2
    UPPER = NB * (NB + 1) // 2
    N2 = NB * NB * Q
    N3 = N2 + UPPER * Q
    SKIP = N2 - LOWER * Q

    def n1(k, c):
        return k * (NB * Q) + c * Q

    def u1(k, c):
        return (k * (k - 1)) * (Q // 2) + c * Q

    def n2(m, i):
        return (m * (m + 1)) * (Q // 2) + i * Q + N2

    def n3(m, i):
        return i * Q + N3 if isinstance(m, int) and m == 0 else (m * (m - 1)) * (Q // 2) + i * Q + (N3 + NB * Q)

    def k2(m):
        return m * -1 + (NB - 1)

    def row2(m):
        return m + NB

    def row3(m):
        return m + 2 * NB

    def k3(m):
        return NB - 1 if isinstance(m, int) and m == 0 else m - 1

    def col3(m, i):
        return i * -1 + (NB - 1) if isinstance(m, int) and m == 0 else i

    ctx = ExitStack()
    with ctx:
        def sb(name, shape, dt=f32):
            return ctx.enter_context(nc.sbuf_tensor(name, shape, dt))

        def pb(name):
            return ctx.enter_context(nc.psum_tensor(name, [P, HALF], f32))

        def sem(name):
            return ctx.enter_context(nc.semaphore(name))

        zr = sb("zr", [P, NB * BLK])
        s1 = sb("s1", [P, NB * BLK])
        ux = sb("ux", [P, NB * BLK])
        o1 = sb("o1", [P, NB * BLK])

        raw = [sb(f"raw{q}", [P, TILE]) for q in range(Q)]
        hi = [sb(f"hi{r}", [P, TILE], f32r) for r in range(2)]
        lo = [sb(f"lo{r}", [P, TILE], f32r) for r in range(2)]
        rhi = [[sb(f"rhi{r}{l}", [P, JB * P], f32r) for l in range(2)] for r in range(2)]
        rlo = [[sb(f"rlo{r}{l}", [P, JB * P], f32r) for l in range(2)] for r in range(2)]

        t1 = sb("t1", [P, HALF])
        t2 = sb("t2", [P, HALF])
        w0 = sb("w0", [P, P])
        w1 = sb("w1", [P, P])
        wsum = sb("wsum", [P, P])
        ident = sb("ident", [P, P])
        rows = sb("rows", [P, P])
        d = sb("d", [P, N // P])
        rsum = sb("rsum", [P, NB * BLK // P])
        deg = sb("deg", [P, BLK // P])
        sq = sb("sq", [P, BLK // P])
        nw = sb("nw", [P, BLK // P])
        low = sb("low", [P, BLK // P])
        onesr = sb("onesr", [P, P], f32r)
        st = sb("st", [P, G, 6])
        ost = w0[:, 0:H * NB * 6]
        mean = sb("mean", [P, G])
        mv = sb("mv", [P, 2])
        zero = sb("zero", [P, BLK // P])

        acc0 = [pb(f"acc0{h}") for h in range(H)]
        acc1 = [pb(f"acc1{h}") for h in range(H)]
        pA = pb("pA")
        pB = pb("pB")
        pC = pb("pC")
        pD = pb("pD")

        loaded = [sem(f"loaded{q}") for q in range(Q)]
        consts_in = sem("consts_in")
        ident_zero = sem("ident_zero")
        ident_ready = sem("ident_ready")
        ones_set = sem("ones_set")
        setup = sem("setup")
        hi_ready = sem("hi_ready")
        tile_split = sem("tile_split")
        tile_multiplied = sem("tile_multiplied")
        banks_free = sem("banks_free")
        xT_in = sem("xT_in")
        y_done = sem("y_done")
        z_ready = sem("z_ready")
        deg_ready = sem("deg_ready")
        deg_root = sem("deg_root")
        deg_step = sem("deg_step")
        low_step = sem("low_step")
        low_ready = sem("low_ready")
        x_in = sem("x_in")
        t1_filled = sem("t1_filled")
        turned = sem("turned")
        pA_read = sem("pA_read")
        upd_step = sem("upd_step")
        var_ready = sem("var_ready")
        var_root = sem("var_root")
        x1_ready = sem("x1_ready")
        x1_stored = sem("x1_stored")
        x1_turned = sem("x1_turned")
        x1T_ready = sem("x1T_ready")
        s1_made = sem("s1_made")
        s1_ready = sem("s1_ready")
        self_added = sem("self_added")
        o_stats = sem("o_stats")
        o_stored = sem("o_stored")
        fin_step = sem("fin_step")
        fin_cols = sem("fin_cols")
        fin_sum = sem("fin_sum")
        fin_stats = sem("fin_stats")
        root_step = sem("root_step")
        fin_root = sem("fin_root")
        fin_var = sem("fin_var")
        fin_norm = sem("fin_norm")
        out_done = sem("out_done")

        block = ctx.enter_context(nc.Block())

        def half(t, k, h):
            return t[:, ds(k * BLK + h * HALF, HALF)]

        def groups(ap):
            return ap.rearrange("p (g f) -> p g f", f=P)

        @block.sync
        def _(sp):
            def load_block(src, k, c, n, first=False):
                for q in range(Q):
                    if not first:
                        sp.wait_ge(tile_split, n + (q + 1 - Q))
                    sp.dma_start(raw[q][:, :], src[k, c, q]).then_inc(loaded[q], 16)

            load_block(adjN, 0, 0, 0, first=True)
            with sp.Fori(1, NB) as c:
                load_block(adjN, 0, c, n1(0, c))
            with sp.Fori(1, NB) as k:
                with sp.Fori(0, k) as c:
                    load_block(adjT, k, c, n1(k, c))
                with sp.Fori(k, NB) as c:
                    load_block(adjN, k, c, n1(k, c))
            load_block(adjT, NB - 1, NB - 1, N2)
            with sp.Fori(1, NB) as m:
                load_block(adjT, k2(m), k2(m), n2(m, 0))
                with sp.Fori(1, m + 1) as i:
                    load_block(adjT, k2(m), i * -1 + NB, n2(m, i))
            with sp.Fori(0, NB) as i:
                load_block(adjT, NB - 1, col3(0, i), n3(0, i))
            with sp.Fori(1, NB) as m:
                with sp.Fori(0, m) as i:
                    load_block(adjT, k3(m), i, n3(m, i))

        @block.gpsimd
        def _(pool):
            pool.dma_start(w0[:, :], W0).then_inc(consts_in, 16)
            pool.dma_start(w1[:, :], W1).then_inc(consts_in, 16)
            pool.dma_start(t1[:, 0:P], Wself).then_inc(consts_in, 16)
            pool.dma_start(rows[:, :], b_rows).then_inc(consts_in, 16)
            pool.dma_start(t2[:, :], xT[:, 0:HALF]).then_inc(xT_in, 16)
            pool.memset(ident[:, :], 0.0).then_inc(ident_zero, 1)
            pool.wait_ge(ident_zero, 1)
            pool.affine_select(out=ident[:, :], in_=ident[:, :], compare_op=ALU.not_equal, fill=1.0,
                               base=0, pattern=[[-1, P]], channel_multiplier=1).then_inc(ident_ready, 1)
            pool.wait_ge(y_done, 1)
            pool.dma_start(t2[:, :], xT[:, HALF:2 * HALF]).then_inc(xT_in, 16)
            with pool.Fori(1, NB) as k:
                for h in range(H):
                    pool.wait_ge(y_done, k * H + h)
                    pool.dma_start(t2[:, :], xT[:, ds(k * BLK + h * HALF, HALF)]).then_inc(xT_in, 16)

            def load_x(m, h, first=False):
                if first:
                    pool.wait_ge(y_done, H * NB)
                else:
                    pool.wait_ge(s1_made, m * H + h)
                pool.dma_start(groups(t2[:, :]),
                               x[ds(k2(m) * BLK + h * HALF, HALF), :]
                               .rearrange("(g p) f -> p g f", p=P)).then_inc(x_in, 16)

            load_x(0, 0, first=True)
            load_x(0, 1)
            with pool.Fori(1, NB) as m:
                for h in range(H):
                    load_x(m, h)
            with pool.Fori(0, NB) as k:
                pool.wait_ge(fin_norm, k + 1)
                pool.dma_start(out[ds(k * BLK, BLK), :].rearrange("(g p) f -> p g f", p=P),
                               groups(zr[:, ds(k * BLK, BLK)])).then_inc(out_done, 16)
            pool.wait_ge(out_done, 16 * NB)

        @block.scalar
        def _(act):
            def split_hi(n, u, c, q, layers, rows_known, first=False):
                r = q % 2
                if not (first and q < 2):
                    act.wait_ge(tile_multiplied, u + (q - 1))
                if q == 0 and rows_known is not None:
                    act.wait_ge(*rows_known)
                for l in layers:
                    src = (zr, s1)[l]
                    nc.scalar.activation(rhi[r][l][:, :], src[:, ds(c * BLK + q * JB * P, JB * P)], ACT.Copy)
                act.wait_ge(loaded[q], n * (16 // Q) + 16)
                nc.scalar.activation(hi[r][:, :], raw[q][:, :], ACT.Copy).then_inc(hi_ready, 1)

            def degree_root(k):
                act.wait_ge(deg_ready, k + 1)
                nc.scalar.activation(sq[:, :], deg[:, :], ACT.Sqrt).then_inc(deg_root, 1)

            degree_root(0)
            for q in range(Q):
                split_hi(n1(1, 0), 0, 0, q, [0], (z_ready, 1), first=True)
            degree_root(1)
            with act.Fori(2, NB) as k:
                with act.Fori(0, k) as c:
                    for q in range(Q):
                        split_hi(n1(k, c), u1(k, c), c, q, [0], (z_ready, c + 1))
                degree_root(k)

            def fill_t1(m, h, first=False):
                g = m * H + h
                act.wait_ge(banks_free, row2(m))
                if not first:
                    act.wait_ge(x1_stored, g)
                nc.scalar.activation(t1[:, :], half(ux, k2(m), h), ACT.Copy).then_inc(t1_filled, 1)

            def root_var(m, h):
                g = m * H + h
                act.wait_ge(var_ready, g + 1)
                nc.scalar.activation(sq[:, 0:G], nw[:, 0:G], ACT.Sqrt).then_inc(var_root, 1)

            def copy_x1T(m, h):
                g = m * H + h
                act.wait_ge(x1_turned, g + 1)
                nc.scalar.activation(t2[:, :], pB[:, :], ACT.Copy).then_inc(x1T_ready, 1)
                nc.scalar.activation(half(ux, k2(m), h), t1[:, :], ACT.Copy).then_inc(x1_stored, 1)

            def copy_s1(m, h):
                g = m * H + h
                act.wait_ge(s1_made, g + 1)
                nc.scalar.activation(half(s1, k2(m), h), pC[:, :], ACT.Copy).then_inc(s1_ready, 1)

            for q in range(Q):
                split_hi(N2, N2 - SKIP, NB - 1, q, [0], (z_ready, NB))

            def diag_hi(m, q):
                split_hi(n2(m, 0), n2(m, 0) - SKIP, k2(m), q, [0], None)

            def dual_hi(m, i, q):
                split_hi(n2(m, i), n2(m, i) - SKIP, i * -1 + NB, q, [0, 1], (s1_ready, i * H))

            def with_update(m, tile, first=False):
                fill_t1(m, 0, first)
                tile(0)
                tile(1)
                root_var(m, 0)
                tile(2)
                copy_x1T(m, 0)
                fill_t1(m, 1)
                tile(3)
                copy_s1(m, 0)
                root_var(m, 1)
                copy_x1T(m, 1)
                copy_s1(m, 1)

            with_update(0, lambda q: diag_hi(1, q), first=True)
            for q in range(Q):
                dual_hi(1, 1, q)
            with act.Fori(2, NB) as m:
                for q in range(Q):
                    diag_hi(m, q)
                with_update(m - 1, lambda q: dual_hi(m, 1, q))
                with act.Fori(2, m + 1) as i:
                    for q in range(Q):
                        dual_hi(m, i, q)

            def single_hi(m, i, q):
                first_row = isinstance(m, int) and m == 0
                split_hi(n3(m, i), n3(m, i) - SKIP, col3(m, i), q, [1],
                         (s1_ready, i * H + H) if first_row else None)

            def relu_half(m, h, first=False):
                g = m * H + h
                act.wait_ge(banks_free, row3(m))
                if first:
                    act.wait_ge(x1_stored, H * NB)
                else:
                    act.wait_ge(turned, g + H * NB)
                    act.wait_ge(o_stats, g)
                nc.scalar.activation(t1[:, :], half(o1, k3(m), h), ACT.Relu).then_inc(t1_filled, 1)

            def store_o(m, h):
                g = m * H + h
                act.wait_ge(turned, g + (H * NB + 1))
                nc.scalar.activation(half(zr, k3(m), h), pA[:, :], ACT.Copy).then_inc(o_stored, 1)

            with_update(NB - 1, lambda q: single_hi(0, 0, q))
            with act.Fori(1, NB) as i:
                for q in range(Q):
                    single_hi(0, i, q)

            def row_with_relu(m, first=False):
                relu_half(m - 1, 0, first)
                single_hi(m, 0, 0)
                store_o(m - 1, 0)
                relu_half(m - 1, 1)
                single_hi(m, 0, 1)
                store_o(m - 1, 1)
                single_hi(m, 0, 2)
                single_hi(m, 0, 3)

            row_with_relu(1, first=True)
            with act.Fori(2, NB) as m:
                row_with_relu(m)
                with act.Fori(1, m) as i:
                    for q in range(Q):
                        single_hi(m, i, q)
            for h in range(H):
                relu_half(NB - 1, h)
                store_o(NB - 1, h)

            act.wait_ge(fin_var, 1)
            nc.scalar.activation(sq[:, 0:1], deg[:, 0:1], ACT.Sqrt).then_inc(fin_root, 1)
            act.wait_ge(fin_var, 2)
            nc.scalar.activation(rsum[:, :], d[:, :], ACT.Sqrt).then_inc(fin_root, 1)

        @block.vector
        def _(dve):
            V = nc.vector

            class Chain:

                def __init__(self, s, base):
                    self.s, self.base, self.count = s, base, 0

                def __call__(self, ins):
                    self.count += 1
                    ins.then_inc(self.s, 1)
                    dve.wait_ge(self.s, self.base + self.count)

            V.memset(o1[:, (NB - 1) * BLK:NB * BLK], 0.0)
            V.memset(ux[:, 0:BLK], 0.0)
            V.memset(onesr[:, :].bitcast(f32), 1.0).then_inc(ones_set, 1)
            V.memset(zero[:, :], 0.0)
            V.memset(rsum[:, :], 0.0).then_inc(setup, 1)
            dve.wait_ge(consts_in, 64)
            V.tensor_add(wsum[:, :], w1[:, :], t1[:, 0:P]).then_inc(setup, 1)
            dve.wait_ge(setup, 2)
            dve.wait_ge(ident_ready, 1)

            def split_lo(n, u, c, q, layers):
                r = q % 2
                dve.wait_ge(hi_ready, u + (q + 1))
                for l in layers:
                    src = (zr, s1)[l]
                    V.tensor_sub(rlo[r][l][:, :], src[:, ds(c * BLK + q * JB * P, JB * P)],
                                 rhi[r][l][:, :].bitcast(f32))
                V.tensor_sub(lo[r][:, :], raw[q][:, :], hi[r][:, :].bitcast(f32)).then_inc(tile_split, 1)

            def sum_rows(k, c):
                for q in range(Q):
                    dve.wait_ge(loaded[q], n1(k, c) * (16 // Q) + 16)
                    V.tensor_reduce(rsum[:, ds(c * (BLK // P) + q * JB, JB)],
                                    raw[q][:, :].rearrange("p (g j) -> p g j", g=JB),
                                    AX.X, ALU.add).then_inc(tile_split, 1)

            DEG_STEPS = 7

            def newton(step, r, v, tmp):
                step(V.tensor_mul(tmp, r, r))
                step(V.tensor_mul(tmp, tmp, v))
                step(V.tensor_scalar(tmp, tmp, -0.5, 1.5, ALU.mult, ALU.add))

            def degrees(k, lower):
                step = Chain(deg_step, k * DEG_STEPS)
                dve.wait_ge(tile_split, k * (NB * Q) + NB * Q)
                step(V.tensor_reduce(deg[:, :], rsum[:, :].rearrange("p (c g) -> p g c", c=NB), AX.X, ALU.add))
                if lower:
                    dve.wait_ge(low_ready, k)
                    step(V.scalar_tensor_tensor(deg[:, :], deg[:, :], 1.0, low[:, :], ALU.add, ALU.add))
                else:
                    step(V.tensor_scalar_add(deg[:, :], deg[:, :], 1.0))
                V.tensor_copy(rsum[:, ds(k * (BLK // P), BLK // P)], zero[:, :]).then_inc(deg_ready, 1)
                dve.wait_ge(deg_root, k + 1)
                dk = d[:, ds(k * (BLK // P), BLK // P)]
                step(V.reciprocal(dk, sq[:, :]))
                newton(step, dk, deg[:, :], nw[:, :])
                step(V.tensor_mul(dk, dk, nw[:, :]))
                for h in range(H):
                    dve.wait_ge(y_done, k * H + (h + 1))
                    last = V.tensor_mul(groups(half(zr, k, h)), groups((pA, pB)[h][:, :]),
                                        d[:, ds(k * (BLK // P) + h * G, G)].unsqueeze(2).to_broadcast([P, G, P]))
                last.then_inc(z_ready, 1)
                assert step.count == DEG_STEPS

            def lower_out(k):
                step = Chain(low_step, (k - 1) * (2 * H - 2))
                dve.wait_ge(tile_multiplied, u1(k + 1, 0))
                for h in range(H):
                    V.tensor_copy(half(ux, k, h), acc0[h][:, :])
                for h in range(H):
                    ins = V.tensor_mul(groups(t1[:, :]), groups(acc1[h][:, :]),
                                       ident[:, :].unsqueeze(1).to_broadcast([P, G, P]))
                    if h == H - 1:
                        ins.then_inc(banks_free, 1)
                        dve.wait_ge(banks_free, k)
                    else:
                        step(ins)
                    ins = V.tensor_reduce(low[:, h * G:h * G + G], groups(t1[:, :]), AX.X, ALU.add)
                    if h == H - 1:
                        ins.then_inc(low_ready, 1)
                    else:
                        step(ins)

            sum_rows(0, 0)
            with dve.Fori(1, NB) as c:
                sum_rows(0, c)
            degrees(0, lower=False)
            for q in range(Q):
                split_lo(n1(1, 0), 0, 0, q, [0])
            lower_out(1)
            with dve.Fori(1, NB) as c:
                sum_rows(1, c)
            degrees(1, lower=True)
            with dve.Fori(2, NB) as k:
                with dve.Fori(0, k) as c:
                    for q in range(Q):
                        split_lo(n1(k, c), u1(k, c), c, q, [0])
                lower_out(k)
                with dve.Fori(k, NB) as c:
                    sum_rows(k, c)
                degrees(k, lower=True)

            def moments(step, six, mean, var, tmp):
                V.tensor_add(mean, six[:, :, 1], six[:, :, 4])
                V.tensor_sub(tmp, six[:, :, 1], six[:, :, 4])
                step(V.tensor_add(var, six[:, :, 2], six[:, :, 5]))
                V.tensor_scalar_mul(mean, mean, 0.5)
                V.scalar_tensor_tensor(tmp, tmp, 0.25, tmp, ALU.mult, ALU.mult)
                step(V.tensor_scalar(var, var, 1.0 / P, EPS_LN, ALU.mult, ALU.add))
                return V.tensor_add(var, var, tmp)

            UPD_STEPS = 11

            def update(m, h):
                g = m * H + h
                k = k2(m)
                t1g = groups(t1[:, :])
                step = Chain(upd_step, g * UPD_STEPS)
                dve.wait_ge(turned, g + 1)
                V.tensor_add(t1[:, :], pA[:, :], half(zr, k, h)).then_inc(pA_read, 1)
                dve.wait_ge(pA_read, g + 1)
                step(V.tensor_mul(t1g, t1g, d[:, ds(k * (BLK // P) + h * G, G)].unsqueeze(2).to_broadcast([P, G, P])))
                step(V.tensor_add(t1g, t1g, rows[:, :].unsqueeze(1).to_broadcast([P, G, P])))
                dve.wait_ge(x_in, g * 16 + 16)
                step(V.scalar_tensor_tensor(t1[:, :], t1[:, :], 0.0, t2[:, :], ALU.max, ALU.add))
                for j in range(G):
                    last = V.bn_stats(st[:, j, :], t1g[:, j, :])
                step(last)
                moments(step, st[:, :, :], mean[:, :], nw[:, 0:G], deg[:, G:2 * G]).then_inc(var_ready, 1)
                dve.wait_ge(var_root, g + 1)
                step(V.reciprocal(deg[:, 0:G], sq[:, 0:G]))
                newton(step, deg[:, 0:G], nw[:, 0:G], deg[:, G:2 * G])
                step(V.tensor_mul(deg[:, 0:G], deg[:, 0:G], deg[:, G:2 * G]))
                for j in range(G):
                    last = V.tensor_scalar(t1g[:, j, :], t1g[:, j, :], mean[:, j:j + 1], deg[:, j:j + 1],
                                           ALU.subtract, ALU.mult)
                last.then_inc(x1_ready, 1)
                assert step.count == UPD_STEPS, step.count

            def add_self(m, h):
                g = m * H + h
                k = k2(m)
                dve.wait_ge(s1_made, g + 1)
                V.tensor_add(half(o1, k, h), half(o1, k, h), pD[:, :]).then_inc(self_added, 1)

            def row_out2(m, dual):
                k = k2(m)
                dve.wait_ge(tile_multiplied, n2(m + 1, 0) - SKIP)
                for h in range(H):
                    last = V.tensor_add(half(ux, k, h), half(ux, k, h), acc0[h][:, :])
                if dual:
                    for h in range(H):
                        last = V.tensor_copy(half(o1, k, h), acc1[h][:, :])
                last.then_inc(banks_free, 1)
                dve.wait_ge(banks_free, row2(m))

            def diag_lo(m, q):
                split_lo(n2(m, 0), n2(m, 0) - SKIP, k2(m), q, [0])

            def dual_lo(m, i, q):
                split_lo(n2(m, i), n2(m, i) - SKIP, i * -1 + NB, q, [0, 1])

            for q in range(Q):
                split_lo(N2, N2 - SKIP, NB - 1, q, [0])
            row_out2(0, dual=False)

            def with_update(m, tile):
                tile(0)
                tile(1)
                update(m, 0)
                tile(2)
                tile(3)
                add_self(m, 0)
                update(m, 1)
                add_self(m, 1)

            with_update(0, lambda q: diag_lo(1, q))
            for q in range(Q):
                dual_lo(1, 1, q)
            row_out2(1, dual=True)
            with dve.Fori(2, NB) as m:
                for q in range(Q):
                    diag_lo(m, q)
                with_update(m - 1, lambda q: dual_lo(m, 1, q))
                with dve.Fori(2, m + 1) as i:
                    for q in range(Q):
                        dual_lo(m, i, q)
                row_out2(m, dual=True)

            def single_lo(m, i, q):
                split_lo(n3(m, i), n3(m, i) - SKIP, col3(m, i), q, [1])

            def row_out3(m):
                k = k3(m)
                dve.wait_ge(tile_multiplied, n3(m + 1, 0) - SKIP)
                for h in range(H):
                    last = V.tensor_add(half(o1, k, h), half(o1, k, h), acc0[h][:, :])
                last.then_inc(banks_free, 1)

            def stats_half(m, h):
                g = m * H + h
                dve.wait_ge(t1_filled, g + (H * NB + 1))
                V.bn_stats(w0[:, ds(g * 6, 6)], t1[:, :]).then_inc(o_stats, 1)

            with_update(NB - 1, lambda q: single_lo(0, 0, q))
            with dve.Fori(1, NB) as i:
                for q in range(Q):
                    single_lo(0, i, q)
            dve.wait_ge(self_added, H * NB)
            row_out3(0)

            def row_with_stats(m):
                single_lo(m, 0, 0)
                stats_half(m - 1, 0)
                single_lo(m, 0, 1)
                stats_half(m - 1, 1)
                single_lo(m, 0, 2)
                single_lo(m, 0, 3)

            row_with_stats(1)
            row_out3(1)
            with dve.Fori(2, NB) as m:
                row_with_stats(m)
                with dve.Fori(1, m) as i:
                    for q in range(Q):
                        single_lo(m, i, q)
                row_out3(m)
            stats_half(NB - 1, 0)
            stats_half(NB - 1, 1)

            fin = Chain(fin_step, 0)
            dve.wait_ge(o_stats, H * NB)
            dve.wait_ge(turned, 2 * H * NB)
            fin(V.bn_aggr(mv[:, :], ost))
            V.memset(t1[:, P:2 * P], 1.0)
            V.tensor_copy(t1[:, 0:P], mv[:, 0:1].to_broadcast([P, P])).then_inc(fin_cols, 1)
            dve.wait_ge(fin_sum, 1)
            fin(V.tensor_copy(rows[:, :], pC[:, 0:P]))
            V.tensor_scalar_add(deg[:, 0:1], pD[:, 0:1], EPS_PN).then_inc(fin_var, 1)
            dve.wait_ge(fin_root, 1)
            rnorm = deg[:, 1:2]
            fin(V.reciprocal(rnorm, sq[:, 0:1]))
            newton(fin, rnorm, deg[:, 0:1], deg[:, 2:3])
            fin(V.tensor_mul(rnorm, rnorm, deg[:, 2:3]))
            dve.wait_ge(o_stored, H * NB)
            FIRST, PER = fin.count, 2
            NG = N // P
            BG = BLK // P
            MEAN, RSTD, TMP = 6 * NG, 7 * NG, 8 * NG
            with dve.Fori(0, NB) as k:
                step = Chain(fin_step, k * PER + FIRST)
                zk = zr[:, ds(k * BLK, BLK)]
                step(V.tensor_sub(groups(zk), groups(zk), rows[:, :].unsqueeze(1).to_broadcast([P, BG, P])))
                step(V.scalar_tensor_tensor(zk, zk, rnorm, ux[:, ds(k * BLK, BLK)], ALU.mult, ALU.add))
                for j in range(BG):
                    last = V.bn_stats(s1[:, ds((k * BG + j) * 6, 6)], zr[:, ds(k * BLK + j * P, P)])
                last.then_inc(fin_stats, 1)
            dve.wait_ge(fin_stats, NB)
            root = Chain(root_step, 0)
            moments(root, s1[:, 0:6 * NG].rearrange("p (g t) -> p g t", t=6), s1[:, MEAN:MEAN + NG], d[:, :],
                    s1[:, TMP:TMP + NG]).then_inc(fin_var, 1)
            dve.wait_ge(fin_root, 2)
            rstd, tmp = s1[:, RSTD:RSTD + NG], s1[:, TMP:TMP + NG]
            root(V.reciprocal(rstd, rsum[:, :]))
            newton(root, rstd, d[:, :], tmp)
            root(V.tensor_mul(rstd, rstd, tmp))
            with dve.Fori(0, NB) as k:
                for j in range(BG):
                    zg = zr[:, ds(k * BLK + j * P, P)]
                    last = V.tensor_scalar(zg, zg, s1[:, ds(k * BG + j + MEAN, 1)],
                                           s1[:, ds(k * BG + j + RSTD, 1)], ALU.subtract, ALU.mult)
                last.then_inc(fin_norm, 1)

        @block.tensor
        def _(pe):
            T = nc.tensor

            def multiply(n, q, layers, first=(), sums=False):
                r = q % 2
                pe.wait_ge(tile_split, n + (q + 1))
                begun = set()
                for j in range(JB):
                    for l, banks in layers:
                        for stat, moving in ((rhi[r][l], (hi[r], lo[r])), (rlo[r][l], (hi[r],))):
                            for h in range(H):
                                for mov in moving:
                                    start = bool(first) and l in first and q == 0 and (l, h) not in begun
                                    begun.add((l, h))
                                    last = T.matmul(banks[h][:, :], stat[:, j * P:j * P + P],
                                                    mov[:, j * BLK + h * HALF:j * BLK + (h + 1) * HALF],
                                                    start=start,
                                                    stop=(q == Q - 1 and j == JB - 1 and stat is rlo[r][l]),
                                                    skip_group_check=True)
                    if sums:
                        for h in range(H):
                            for mov in (hi[r], lo[r]):
                                start = bool(first) and q == 0 and ("sum", h) not in begun
                                begun.add(("sum", h))
                                last = T.matmul(acc1[h][:, :], onesr[:, :],
                                                mov[:, j * BLK + h * HALF:j * BLK + (h + 1) * HALF],
                                                start=start, stop=(q == Q - 1 and j == JB - 1 and mov is lo[r]),
                                                skip_group_check=True)
                last.then_inc(tile_multiplied, 1)

            def first_product(k, h):
                pe.wait_ge(xT_in, (k * H + h) * 16 + 16)
                for g in range(G):
                    last = T.matmul((pA, pB)[h][:, g * P:g * P + P], t2[:, g * P:g * P + P], w0[:, :],
                                    start=True, stop=True)
                last.then_inc(y_done, 1)

            pe.wait_ge(consts_in, 64)
            pe.wait_ge(ones_set, 1)
            for h in range(H):
                first_product(0, h)
            pe.wait_ge(z_ready, 1)
            for h in range(H):
                first_product(1, h)
            for q in range(Q):
                multiply(n1(1, 0), q, [(0, acc0)], first=[0], sums=True)
            with pe.Fori(2, NB) as k:
                pe.wait_ge(z_ready, k)
                for h in range(H):
                    first_product(k, h)
                pe.wait_ge(banks_free, k - 1)
                for q in range(Q):
                    multiply(n1(k, 0), q, [(0, acc0)], first=[0], sums=True)
                with pe.Fori(1, k) as c:
                    for q in range(Q):
                        multiply(n1(k, c), q, [(0, acc0)], sums=True)

            def turn_sum(m, h, first=False):
                g = m * H + h
                pe.wait_ge(t1_filled, g + 1)
                if not first:
                    pe.wait_ge(pA_read, g)
                for j in range(G):
                    last = T.transpose(pA[:, j * P:j * P + P], t1[:, j * P:j * P + P], ident[:, :])
                last.then_inc(turned, 1)

            def turn_x1(m, h, first=False):
                g = m * H + h
                pe.wait_ge(x1_ready, g + 1)
                if not first:
                    pe.wait_ge(x1T_ready, g)
                for j in range(G):
                    last = T.transpose(pB[:, j * P:j * P + P], t1[:, j * P:j * P + P], ident[:, :])
                last.then_inc(x1_turned, 1)

            def make_s1(m, h, first=False):
                g = m * H + h
                pe.wait_ge(x1T_ready, g + 1)
                if not first:
                    pe.wait_ge(s1_ready, g)
                    pe.wait_ge(self_added, g)
                for j in range(G):
                    T.matmul(pC[:, j * P:j * P + P], t2[:, j * P:j * P + P], w1[:, :], start=True, stop=True)
                T.matmul(pD[:, :], wsum[:, :], t2[:, :], start=True, stop=True).then_inc(s1_made, 1)

            def with_update(m, tile, first=False):
                turn_sum(m, 0, first)
                tile(0)
                tile(1)
                turn_x1(m, 0, first)
                tile(2)
                make_s1(m, 0, first)
                turn_sum(m, 1)
                tile(3)
                turn_x1(m, 1)
                make_s1(m, 1)

            L0, L1 = (0, acc0), (1, acc1)

            def diag(m, q):
                multiply(n2(m, 0), q, [L0], first=[0])

            def dual(m, i, q, first=()):
                multiply(n2(m, i), q, [L0, L1], first=first)

            pe.wait_ge(setup, 2)
            pe.wait_ge(banks_free, NB - 1)
            for q in range(Q):
                diag(0, q)
            pe.wait_ge(banks_free, row2(0))
            with_update(0, lambda q: diag(1, q), first=True)
            for q in range(Q):
                dual(1, 1, q, first=[1])
            with pe.Fori(2, NB) as m:
                pe.wait_ge(banks_free, row2(m - 1))
                for q in range(Q):
                    diag(m, q)
                with_update(m - 1, lambda q: dual(m, 1, q, first=[1]))
                with pe.Fori(2, m + 1) as i:
                    for q in range(Q):
                        dual(m, i, q)

            L3 = (1, acc0)

            def single(m, i, q, first=()):
                multiply(n3(m, i), q, [L3], first=first)

            def turn_o(m, h, first=False):
                g = m * H + h
                pe.wait_ge(t1_filled, g + (H * NB + 1))
                if first:
                    pe.wait_ge(pA_read, H * NB)
                else:
                    pe.wait_ge(o_stored, g)
                for j in range(G):
                    last = T.transpose(pA[:, j * P:j * P + P], t1[:, j * P:j * P + P], ident[:, :])
                last.then_inc(turned, 1)

            def row_with_turn(m, first=False):
                single(m, 0, 0, first=[1])
                turn_o(m - 1, 0, first)
                single(m, 0, 1)
                turn_o(m - 1, 1)
                single(m, 0, 2)
                single(m, 0, 3)

            pe.wait_ge(banks_free, row2(NB - 1))
            with_update(NB - 1, lambda q: single(0, 0, q, first=[1]))
            with pe.Fori(1, NB) as i:
                for q in range(Q):
                    single(0, i, q)
            pe.wait_ge(banks_free, row3(0))
            row_with_turn(1, first=True)
            with pe.Fori(2, NB) as m:
                pe.wait_ge(banks_free, row3(m - 1))
                row_with_turn(m)
                with pe.Fori(1, m) as i:
                    for q in range(Q):
                        single(m, i, q)
            for h in range(H):
                turn_o(NB - 1, h)

            pe.wait_ge(fin_cols, 1)
            T.matmul(pC[:, 0:P], t1[:, 0:P], ident[:, :], start=True, stop=True)
            T.matmul(pD[:, 0:1], t1[:, P:2 * P], mv[:, 1:2], start=True, stop=True).then_inc(fin_sum, 1)


def kernel(x, adj, L0_gnn_W, L0_gnn_b, L1_gnn_weight, L1_gnn_self_weight):
    import numpy as np
    import concourse.bacc as bacc
    from concourse.bass_utils import run_bass_kernel_spmd

    x, adj = np.asarray(x), np.asarray(adj)
    n, f = x.shape
    nb, q, jb = n // 1024, 4, 2
    blocks = adj.reshape(nb, 1024, nb, 1024)
    adj_t = np.ascontiguousarray(
        blocks.reshape(nb, 1024, nb, q, jb, 128).transpose(0, 2, 3, 5, 4, 1)).reshape(nb, nb, q, 128, jb * 1024)
    adj_n = np.ascontiguousarray(
        blocks.reshape(nb, q, jb, 128, nb, 1024).transpose(0, 4, 1, 3, 2, 5)).reshape(nb, nb, q, 128, jb * 1024)
    arrays = {
        "x": np.ascontiguousarray(x),
        "xT": np.ascontiguousarray(x.T),
        "adjT": adj_t,
        "adjN": adj_n,
        "W0": np.ascontiguousarray(L0_gnn_W),
        "b_rows": np.ascontiguousarray(np.broadcast_to(np.asarray(L0_gnn_b)[None, :], (128, f))),
        "W1": np.ascontiguousarray(L1_gnn_weight),
        "Wself": np.ascontiguousarray(L1_gnn_self_weight),
    }
    nc = bacc.Bacc("TRN2", target_bir_lowering=False, num_devices=1)
    f32 = mybir.dt.float32
    args = [nc.dram_tensor(f"in_{name}", a.shape, f32, kind="ExternalInput").ap() for name, a in arrays.items()]
    out = nc.dram_tensor("out", (n, f), f32, kind="ExternalOutput").ap()
    graph_kernel(nc, *args, out)
    r = run_bass_kernel_spmd(nc, [{f"in_{name}": a for name, a in arrays.items()}], core_ids=[0])
    return r.results[0]["out"]
```

```python
import concourse.bass as bass
from concourse import mybir
from contextlib import ExitStack


def graph_kernel(nc, x, xT, adjT, adjN, W0, b_rows, W1, Wself, out):
    f32 = mybir.dt.float32
    f32r = mybir.dt.float32r
    ACT = mybir.ActivationFunctionType
    ALU = mybir.AluOpType
    AX = mybir.AxisListType
    ds = bass.ds

    P = 128
    N = x.shape[0]
    F = x.shape[1]
    assert F == P
    BLK = 1024
    NB = N // BLK
    Q = 4
    JB = BLK // Q // P
    TILE = JB * BLK
    H = BLK // 512
    HALF = 512
    G = HALF // P
    EPS_LN = 1e-5
    EPS_PN = 1e-6
    assert NB >= 4 and JB == 2 and H == 2

    S = Q * JB
    LOWER = NB * (NB - 1) // 2
    UPPER = NB * (NB + 1) // 2
    N2 = NB * NB * S
    N3 = N2 + UPPER * S
    SKIP = N2 - (LOWER + 1) * S

    def n1(k, c):
        return k * (NB * S) + c * S

    def n1_pair(k, i):
        return k * (NB * S) + i * (2 * S)

    def n1_rest(k, i):
        return k * ((NB - 2) * S) + i * S + 2 * NB * S

    def u1(k, c):
        return (k * (k - 1)) * (S // 2) + c * S + S

    def u1_rest(k, i):
        return (k * (k - 3)) * (S // 2) + i * S + (NB + 1) * S

    def within(v):
        return v if isinstance(v, int) else v.with_bounds(min_val=0, max_val=NB - 1)

    def phase1_rows(eng, row):
        with eng.Fori(1, NB // 2) as k:
            row(k, "few")
        row(NB // 2, "half")
        with eng.Fori(NB // 2 + 1, NB) as k:
            row(k, "many")

    def phase1_blocks(eng, k, kind, pair, natural, lower):
        if kind == "few":
            with eng.Fori(0, k) as i:
                pair(k, i)
            if natural:
                with eng.Fori(k * 2, NB) as c:
                    natural(k, c)
        elif kind == "half":
            with eng.Fori(0, NB // 2) as i:
                pair(k, i)
        else:
            with eng.Fori(0, k * -1 + NB) as i:
                pair(k, i)
            with eng.Fori(0, k * 2 - NB) as i:
                lower(k, i)

    def n2(m, i):
        return (m * (m + 1)) * (S // 2) + i * S + N2

    def n3(m, i):
        return i * S + N3 if isinstance(m, int) and m == 0 else (m * (m - 1)) * (S // 2) + i * S + (N3 + NB * S)

    def k2(m):
        return m * -1 + (NB - 1)

    def row2(m):
        return m + NB

    def row3(m):
        return m + 2 * NB

    def k3(m):
        return NB - 1 if isinstance(m, int) and m == 0 else m - 1

    def col3(m, i):
        return i * -1 + (NB - 1) if isinstance(m, int) and m == 0 else i

    ctx = ExitStack()
    with ctx:
        def sb(name, shape, dt=f32):
            return ctx.enter_context(nc.sbuf_tensor(name, shape, dt))

        def pb(name):
            return ctx.enter_context(nc.psum_tensor(name, [P, HALF], f32))

        def sem(name):
            return ctx.enter_context(nc.semaphore(name))

        zr = sb("zr", [P, NB * BLK])
        s1 = sb("s1", [P, NB * BLK])
        ux = sb("ux", [P, NB * BLK])
        o1 = sb("o1", [P, NB * BLK])

        raw = [sb(f"raw{q}", [P, TILE]) for q in range(Q)]
        hi = [sb(f"hi{r}", [P, BLK], f32r) for r in range(2 * JB)]
        lo = [sb(f"lo{r}", [P, BLK], f32r) for r in range(2 * JB)]
        rhi = [[sb(f"rhi{r}{l}", [P, JB * P], f32r) for l in range(2)] for r in range(2)]
        rlo = [[sb(f"rlo{r}{l}", [P, JB * P], f32r) for l in range(2)] for r in range(2)]

        t1 = sb("t1", [P, HALF])
        t2 = sb("t2", [P, HALF])
        w0 = sb("w0", [P, P])
        w1 = sb("w1", [P, P])
        wsum = sb("wsum", [P, P])
        ident = sb("ident", [P, P])
        rows = sb("rows", [P, P])
        d = sb("d", [P, N // P])
        rsum = sb("rsum", [P, NB * BLK // P])
        deg = sb("deg", [P, BLK // P])
        sq = sb("sq", [P, BLK // P])
        nw = sb("nw", [P, BLK // P])
        low = sb("low", [P, BLK // P])
        onesr = sb("onesr", [P, P], f32r)
        st = sb("st", [P, G, 6])
        ost = w0[:, 0:H * NB * 6]
        mean = sb("mean", [P, G])
        mv = sb("mv", [P, 2])
        zero = sb("zero", [P, BLK // P])

        acc0 = [pb(f"acc0{h}") for h in range(H)]
        acc1 = [pb(f"acc1{h}") for h in range(H)]
        pA = pb("pA")
        pB = pb("pB")
        pC = pb("pC")
        pD = pb("pD")

        loaded = [sem(f"loaded{q}") for q in range(Q)]
        consts_in = sem("consts_in")
        ident_zero = sem("ident_zero")
        ident_ready = sem("ident_ready")
        ones_set = sem("ones_set")
        setup = sem("setup")
        hi_ready = sem("hi_ready")
        slice_split = sem("slice_split")
        slice_multiplied = sem("slice_multiplied")
        banks_free = sem("banks_free")
        xT_in = sem("xT_in")
        y_done = sem("y_done")
        z_ready = sem("z_ready")
        deg_ready = sem("deg_ready")
        deg_root = sem("deg_root")
        deg_step = sem("deg_step")
        low_step = sem("low_step")
        low_ready = sem("low_ready")
        x_in = sem("x_in")
        t1_filled = sem("t1_filled")
        turned = sem("turned")
        pA_read = sem("pA_read")
        upd_step = sem("upd_step")
        var_ready = sem("var_ready")
        var_root = sem("var_root")
        x1_ready = sem("x1_ready")
        x1_stored = sem("x1_stored")
        x1_turned = sem("x1_turned")
        x1T_ready = sem("x1T_ready")
        s1_made = sem("s1_made")
        s1_ready = sem("s1_ready")
        self_added = sem("self_added")
        o_stats = sem("o_stats")
        o_stored = sem("o_stored")
        fin_step = sem("fin_step")
        fin_cols = sem("fin_cols")
        fin_sum = sem("fin_sum")
        fin_stats = sem("fin_stats")
        root_step = sem("root_step")
        fin_root = sem("fin_root")
        fin_var = sem("fin_var")
        fin_norm = sem("fin_norm")
        out_done = sem("out_done")

        block = ctx.enter_context(nc.Block())

        def half(t, k, h):
            return t[:, ds(k * BLK + h * HALF, HALF)]

        def groups(ap):
            return ap.rearrange("p (g f) -> p g f", f=P)

        @block.sync
        def _(sp):
            def load_tile(src, k, c, q, n, o, first=False):
                if not first:
                    sp.wait_ge(slice_split, n + (o + 1 - Q) * JB)
                sp.dma_start(raw[o % Q][:, :], src[k, c, q]).then_inc(loaded[o % Q], 16)

            def load_block(src, k, c, n, first=False):
                for q in range(Q):
                    load_tile(src, k, c, q, n, q, first)

            def load_pair(k, i):
                for q in range(Q):
                    load_tile(adjT, k, i, q, n1_pair(k, i), 2 * q)
                    load_tile(adjN, k, within(k + i), q, n1_pair(k, i), 2 * q + 1)

            load_block(adjN, 0, 0, 0, first=True)
            with sp.Fori(1, NB) as c:
                load_block(adjN, 0, c, n1(0, c))
            phase1_rows(sp, lambda k, kind: phase1_blocks(
                sp, k, kind, load_pair,
                lambda k, c: load_block(adjN, k, c, n1(k, c)),
                lambda k, i: load_block(adjT, k, within(i + (k * -1 + NB)), n1_rest(k, i))))
            load_block(adjT, NB - 1, NB - 1, N2)
            with sp.Fori(1, NB) as m:
                load_block(adjT, k2(m), k2(m), n2(m, 0))
                with sp.Fori(1, m + 1) as i:
                    load_block(adjT, k2(m), i * -1 + NB, n2(m, i))
            with sp.Fori(0, NB) as i:
                load_block(adjT, NB - 1, col3(0, i), n3(0, i))
            with sp.Fori(1, NB) as m:
                with sp.Fori(0, m) as i:
                    load_block(adjT, k3(m), i, n3(m, i))

        @block.gpsimd
        def _(pool):
            pool.dma_start(w0[:, :], W0).then_inc(consts_in, 16)
            pool.dma_start(w1[:, :], W1).then_inc(consts_in, 16)
            pool.dma_start(t1[:, 0:P], Wself).then_inc(consts_in, 16)
            pool.dma_start(rows[:, :], b_rows).then_inc(consts_in, 16)
            pool.dma_start(t2[:, :], xT[:, 0:HALF]).then_inc(xT_in, 16)
            pool.memset(ident[:, :], 0.0).then_inc(ident_zero, 1)
            pool.wait_ge(ident_zero, 1)
            pool.affine_select(out=ident[:, :], in_=ident[:, :], compare_op=ALU.not_equal, fill=1.0,
                               base=0, pattern=[[-1, P]], channel_multiplier=1).then_inc(ident_ready, 1)
            pool.wait_ge(y_done, 1)
            pool.dma_start(t2[:, :], xT[:, HALF:2 * HALF]).then_inc(xT_in, 16)
            with pool.Fori(1, NB) as k:
                for h in range(H):
                    pool.wait_ge(y_done, k * H + h)
                    pool.dma_start(t2[:, :], xT[:, ds(k * BLK + h * HALF, HALF)]).then_inc(xT_in, 16)

            def load_x(m, h, first=False):
                if first:
                    pool.wait_ge(y_done, H * NB)
                else:
                    pool.wait_ge(s1_made, m * H + h)
                pool.dma_start(groups(t2[:, :]),
                               x[ds(k2(m) * BLK + h * HALF, HALF), :]
                               .rearrange("(g p) f -> p g f", p=P)).then_inc(x_in, 16)

            load_x(0, 0, first=True)
            load_x(0, 1)
            with pool.Fori(1, NB) as m:
                for h in range(H):
                    load_x(m, h)
            with pool.Fori(0, NB) as k:
                pool.wait_ge(fin_norm, k + 1)
                pool.dma_start(out[ds(k * BLK, BLK), :].rearrange("(g p) f -> p g f", p=P),
                               groups(zr[:, ds(k * BLK, BLK)])).then_inc(out_done, 16)
            pool.wait_ge(out_done, 16 * NB)

        @block.scalar
        def _(act):
            def split_hi(n, o, u, c, q, layers, rows_known, single=True):
                act.wait_ge(slice_multiplied, u + (q * JB - 3 * JB if single else q * JB - JB))
                if rows_known is not None:
                    act.wait_ge(*rows_known)
                for l in layers:
                    src = (zr, s1)[l]
                    nc.scalar.activation(rhi[q % 2][q // 2 if single else l][:, :],
                                         src[:, ds(c * BLK + q * JB * P, JB * P)], ACT.Copy)
                act.wait_ge(loaded[o % Q], n * (16 // S) + 16 * (o // Q + 1))
                for j in range(JB):
                    act.wait_ge(slice_multiplied, u + (q - 2) * JB + (j + 1))
                    nc.scalar.activation(hi[q % 2 * JB + j][:, :], raw[o % Q][:, j * BLK:(j + 1) * BLK],
                                         ACT.Copy).then_inc(hi_ready, 1)

            def degree_root(k):
                act.wait_ge(deg_ready, k + 1)
                nc.scalar.activation(sq[:, :], deg[:, :], ACT.Sqrt).then_inc(deg_root, 1)

            def lower_hi(k, i):
                for q in range(Q):
                    split_hi(n1_rest(k, i), q, u1_rest(k, i), within(i + (k * -1 + NB)), q, [0], (z_ready, k))

            def pair_hi(k, i):
                for q in range(Q):
                    split_hi(n1_pair(k, i), 2 * q, u1(k, i), i, q, [0], (z_ready, i + 1))

            def row1(k, kind):
                phase1_blocks(act, k, kind, pair_hi, None, lower_hi)
                degree_root(k)

            degree_root(0)
            phase1_rows(act, row1)

            def fill_t1(m, h, first=False):
                g = m * H + h
                act.wait_ge(banks_free, row2(m))
                if not first:
                    act.wait_ge(x1_stored, g)
                nc.scalar.activation(t1[:, :], half(ux, k2(m), h), ACT.Copy).then_inc(t1_filled, 1)

            def root_var(m, h):
                g = m * H + h
                act.wait_ge(var_ready, g + 1)
                nc.scalar.activation(sq[:, 0:G], nw[:, 0:G], ACT.Sqrt).then_inc(var_root, 1)

            def copy_x1T(m, h):
                g = m * H + h
                act.wait_ge(x1_turned, g + 1)
                nc.scalar.activation(t2[:, :], pB[:, :], ACT.Copy).then_inc(x1T_ready, 1)
                nc.scalar.activation(half(ux, k2(m), h), t1[:, :], ACT.Copy).then_inc(x1_stored, 1)

            def copy_s1(m, h):
                g = m * H + h
                act.wait_ge(s1_made, g + 1)
                nc.scalar.activation(half(s1, k2(m), h), pC[:, :], ACT.Copy).then_inc(s1_ready, 1)

            for q in range(Q):
                split_hi(N2, q, N2 - SKIP, NB - 1, q, [0], (z_ready, NB), single=False)

            def diag_hi(m, q):
                split_hi(n2(m, 0), q, n2(m, 0) - SKIP, k2(m), q, [0], None, single=False)

            def dual_hi(m, i, q):
                split_hi(n2(m, i), q, n2(m, i) - SKIP, i * -1 + NB, q, [0, 1], (s1_ready, i * H), single=False)

            def with_update(m, tile, first=False):
                fill_t1(m, 0, first)
                tile(0)
                tile(1)
                root_var(m, 0)
                tile(2)
                copy_x1T(m, 0)
                fill_t1(m, 1)
                tile(3)
                copy_s1(m, 0)
                root_var(m, 1)
                copy_x1T(m, 1)
                copy_s1(m, 1)

            with_update(0, lambda q: diag_hi(1, q), first=True)
            for q in range(Q):
                dual_hi(1, 1, q)
            with act.Fori(2, NB) as m:
                for q in range(Q):
                    diag_hi(m, q)
                with_update(m - 1, lambda q: dual_hi(m, 1, q))
                with act.Fori(2, m + 1) as i:
                    for q in range(Q):
                        dual_hi(m, i, q)

            def single_hi(m, i, q, single=True):
                first_row = isinstance(m, int) and m == 0
                split_hi(n3(m, i), q, n3(m, i) - SKIP, col3(m, i), q, [1],
                         (s1_ready, i * H + H) if first_row else None, single)

            def relu_half(m, h, first=False):
                g = m * H + h
                act.wait_ge(banks_free, row3(m))
                if first:
                    act.wait_ge(x1_stored, H * NB)
                else:
                    act.wait_ge(turned, g + H * NB)
                    act.wait_ge(o_stats, g)
                nc.scalar.activation(t1[:, :], half(o1, k3(m), h), ACT.Relu).then_inc(t1_filled, 1)

            def store_o(m, h):
                g = m * H + h
                act.wait_ge(turned, g + (H * NB + 1))
                nc.scalar.activation(half(zr, k3(m), h), pA[:, :], ACT.Copy).then_inc(o_stored, 1)

            with_update(NB - 1, lambda q: single_hi(0, 0, q, single=False))
            with act.Fori(1, NB) as i:
                for q in range(Q):
                    single_hi(0, i, q)

            def row_with_relu(m, first=False):
                relu_half(m - 1, 0, first)
                single_hi(m, 0, 0)
                store_o(m - 1, 0)
                relu_half(m - 1, 1)
                single_hi(m, 0, 1)
                store_o(m - 1, 1)
                single_hi(m, 0, 2)
                single_hi(m, 0, 3)

            row_with_relu(1, first=True)
            with act.Fori(2, NB) as m:
                row_with_relu(m)
                with act.Fori(1, m) as i:
                    for q in range(Q):
                        single_hi(m, i, q)
            for h in range(H):
                relu_half(NB - 1, h)
                store_o(NB - 1, h)

            act.wait_ge(fin_var, 1)
            nc.scalar.activation(sq[:, 0:1], deg[:, 0:1], ACT.Sqrt).then_inc(fin_root, 1)
            act.wait_ge(fin_var, 2)
            nc.scalar.activation(rsum[:, :], d[:, :], ACT.Sqrt).then_inc(fin_root, 1)

        @block.vector
        def _(dve):
            V = nc.vector

            class Chain:

                def __init__(self, s, base):
                    self.s, self.base, self.count = s, base, 0

                def __call__(self, ins):
                    self.count += 1
                    ins.then_inc(self.s, 1)
                    dve.wait_ge(self.s, self.base + self.count)

            V.memset(o1[:, (NB - 1) * BLK:NB * BLK], 0.0)
            V.memset(ux[:, 0:BLK], 0.0)
            V.memset(onesr[:, :].bitcast(f32), 1.0).then_inc(ones_set, 1)
            V.memset(zero[:, :], 0.0).then_inc(slice_multiplied, S)
            V.memset(rsum[:, :], 0.0).then_inc(setup, 1)
            dve.wait_ge(consts_in, 64)
            V.tensor_add(wsum[:, :], w1[:, :], t1[:, 0:P]).then_inc(setup, 1)
            dve.wait_ge(setup, 2)
            dve.wait_ge(ident_ready, 1)

            def split_lo(n, o, u, c, q, layers, single=True):
                for j in range(JB):
                    dve.wait_ge(hi_ready, u + (q * JB + j + 1 - S))
                    if j == 0:
                        for l in layers:
                            src, p = (zr, s1)[l], q // 2 if single else l
                            V.tensor_sub(rlo[q % 2][p][:, :], src[:, ds(c * BLK + q * JB * P, JB * P)],
                                         rhi[q % 2][p][:, :].bitcast(f32))
                    r = q % 2 * JB + j
                    V.tensor_sub(lo[r][:, :], raw[o % Q][:, j * BLK:(j + 1) * BLK],
                                 hi[r][:, :].bitcast(f32)).then_inc(slice_split, 1)

            def sum_tile(c, q, n, o):
                dve.wait_ge(loaded[o % Q], n * (16 // S) + 16 * (o // Q + 1))
                V.tensor_reduce(rsum[:, ds(c * (BLK // P) + q * JB, JB)],
                                raw[o % Q][:, :].rearrange("p (g j) -> p g j", g=JB),
                                AX.X, ALU.add).then_inc(slice_split, JB)

            def sum_rows(k, c):
                for q in range(Q):
                    sum_tile(c, q, n1(k, c), q)

            DEG_STEPS = 7

            def newton(step, r, v, tmp):
                step(V.tensor_mul(tmp, r, r))
                step(V.tensor_mul(tmp, tmp, v))
                step(V.tensor_scalar(tmp, tmp, -0.5, 1.5, ALU.mult, ALU.add))

            def degrees(k, lower):
                step = Chain(deg_step, k * DEG_STEPS)
                dve.wait_ge(slice_split, k * (NB * S) + NB * S)
                step(V.tensor_reduce(deg[:, :], rsum[:, :].rearrange("p (c g) -> p g c", c=NB), AX.X, ALU.add))
                if lower:
                    dve.wait_ge(low_ready, k)
                    step(V.scalar_tensor_tensor(deg[:, :], deg[:, :], 1.0, low[:, :], ALU.add, ALU.add))
                else:
                    step(V.tensor_scalar_add(deg[:, :], deg[:, :], 1.0))
                V.tensor_copy(rsum[:, ds(k * (BLK // P), BLK // P)], zero[:, :]).then_inc(deg_ready, 1)
                dve.wait_ge(deg_root, k + 1)
                dk = d[:, ds(k * (BLK // P), BLK // P)]
                step(V.reciprocal(dk, sq[:, :]))
                newton(step, dk, deg[:, :], nw[:, :])
                step(V.tensor_mul(dk, dk, nw[:, :]))
                for h in range(H):
                    dve.wait_ge(y_done, k * H + (h + 1))
                    last = V.tensor_mul(groups(half(zr, k, h)), groups((pA, pB)[h][:, :]),
                                        d[:, ds(k * (BLK // P) + h * G, G)].unsqueeze(2).to_broadcast([P, G, P]))
                last.then_inc(z_ready, 1)
                assert step.count == DEG_STEPS

            def lower_out(k):
                step = Chain(low_step, (k - 1) * (2 * H - 2))
                dve.wait_ge(slice_multiplied, u1(k + 1, 0))
                for h in range(H):
                    V.tensor_copy(half(ux, k, h), acc0[h][:, :])
                for h in range(H):
                    ins = V.tensor_mul(groups(t1[:, :]), groups(acc1[h][:, :]),
                                       ident[:, :].unsqueeze(1).to_broadcast([P, G, P]))
                    if h == H - 1:
                        ins.then_inc(banks_free, 1)
                        dve.wait_ge(banks_free, k)
                    else:
                        step(ins)
                    ins = V.tensor_reduce(low[:, h * G:h * G + G], groups(t1[:, :]), AX.X, ALU.add)
                    if h == H - 1:
                        ins.then_inc(low_ready, 1)
                    else:
                        step(ins)

            sum_rows(0, 0)
            with dve.Fori(1, NB) as c:
                sum_rows(0, c)
            degrees(0, lower=False)

            def pair_lo(k, i):
                for q in range(Q):
                    split_lo(n1_pair(k, i), 2 * q, u1(k, i), i, q, [0])
                    sum_tile(within(k + i), q, n1_pair(k, i), 2 * q + 1)

            def lower_lo(k, i):
                for q in range(Q):
                    split_lo(n1_rest(k, i), q, u1_rest(k, i), within(i + (k * -1 + NB)), q, [0])

            def row1(k, kind):
                phase1_blocks(dve, k, kind, pair_lo, sum_rows, lower_lo)
                lower_out(k)
                degrees(k, lower=True)

            phase1_rows(dve, row1)

            def moments(step, six, mean, var, tmp):
                V.tensor_add(mean, six[:, :, 1], six[:, :, 4])
                V.tensor_sub(tmp, six[:, :, 1], six[:, :, 4])
                step(V.tensor_add(var, six[:, :, 2], six[:, :, 5]))
                V.tensor_scalar_mul(mean, mean, 0.5)
                V.scalar_tensor_tensor(tmp, tmp, 0.25, tmp, ALU.mult, ALU.mult)
                step(V.tensor_scalar(var, var, 1.0 / P, EPS_LN, ALU.mult, ALU.add))
                return V.tensor_add(var, var, tmp)

            UPD_STEPS = 11

            def update(m, h):
                g = m * H + h
                k = k2(m)
                t1g = groups(t1[:, :])
                step = Chain(upd_step, g * UPD_STEPS)
                dve.wait_ge(turned, g + 1)
                V.tensor_add(t1[:, :], pA[:, :], half(zr, k, h)).then_inc(pA_read, 1)
                dve.wait_ge(pA_read, g + 1)
                step(V.tensor_mul(t1g, t1g, d[:, ds(k * (BLK // P) + h * G, G)].unsqueeze(2).to_broadcast([P, G, P])))
                step(V.tensor_add(t1g, t1g, rows[:, :].unsqueeze(1).to_broadcast([P, G, P])))
                dve.wait_ge(x_in, g * 16 + 16)
                step(V.scalar_tensor_tensor(t1[:, :], t1[:, :], 0.0, t2[:, :], ALU.max, ALU.add))
                for j in range(G):
                    last = V.bn_stats(st[:, j, :], t1g[:, j, :])
                step(last)
                moments(step, st[:, :, :], mean[:, :], nw[:, 0:G], deg[:, G:2 * G]).then_inc(var_ready, 1)
                dve.wait_ge(var_root, g + 1)
                step(V.reciprocal(deg[:, 0:G], sq[:, 0:G]))
                newton(step, deg[:, 0:G], nw[:, 0:G], deg[:, G:2 * G])
                step(V.tensor_mul(deg[:, 0:G], deg[:, 0:G], deg[:, G:2 * G]))
                for j in range(G):
                    last = V.tensor_scalar(t1g[:, j, :], t1g[:, j, :], mean[:, j:j + 1], deg[:, j:j + 1],
                                           ALU.subtract, ALU.mult)
                last.then_inc(x1_ready, 1)
                assert step.count == UPD_STEPS, step.count

            def add_self(m, h):
                g = m * H + h
                k = k2(m)
                dve.wait_ge(s1_made, g + 1)
                V.tensor_add(half(o1, k, h), half(o1, k, h), pD[:, :]).then_inc(self_added, 1)

            def row_out2(m, dual):
                k = k2(m)
                dve.wait_ge(slice_multiplied, n2(m + 1, 0) - SKIP)
                for h in range(H):
                    last = V.tensor_add(half(ux, k, h), half(ux, k, h), acc0[h][:, :])
                if dual:
                    for h in range(H):
                        last = V.tensor_copy(half(o1, k, h), acc1[h][:, :])
                last.then_inc(banks_free, 1)
                dve.wait_ge(banks_free, row2(m))

            def diag_lo(m, q):
                split_lo(n2(m, 0), q, n2(m, 0) - SKIP, k2(m), q, [0], single=False)

            def dual_lo(m, i, q):
                split_lo(n2(m, i), q, n2(m, i) - SKIP, i * -1 + NB, q, [0, 1], single=False)

            for q in range(Q):
                split_lo(N2, q, N2 - SKIP, NB - 1, q, [0], single=False)
            row_out2(0, dual=False)

            def with_update(m, tile):
                tile(0)
                tile(1)
                update(m, 0)
                tile(2)
                tile(3)
                add_self(m, 0)
                update(m, 1)
                add_self(m, 1)

            with_update(0, lambda q: diag_lo(1, q))
            for q in range(Q):
                dual_lo(1, 1, q)
            row_out2(1, dual=True)
            with dve.Fori(2, NB) as m:
                for q in range(Q):
                    diag_lo(m, q)
                with_update(m - 1, lambda q: dual_lo(m, 1, q))
                with dve.Fori(2, m + 1) as i:
                    for q in range(Q):
                        dual_lo(m, i, q)
                row_out2(m, dual=True)

            def single_lo(m, i, q, single=True):
                split_lo(n3(m, i), q, n3(m, i) - SKIP, col3(m, i), q, [1], single)

            def row_out3(m):
                k = k3(m)
                dve.wait_ge(slice_multiplied, n3(m + 1, 0) - SKIP)
                for h in range(H):
                    last = V.tensor_add(half(o1, k, h), half(o1, k, h), acc0[h][:, :])
                last.then_inc(banks_free, 1)

            def stats_half(m, h):
                g = m * H + h
                dve.wait_ge(t1_filled, g + (H * NB + 1))
                V.bn_stats(w0[:, ds(g * 6, 6)], t1[:, :]).then_inc(o_stats, 1)

            with_update(NB - 1, lambda q: single_lo(0, 0, q, single=False))
            with dve.Fori(1, NB) as i:
                for q in range(Q):
                    single_lo(0, i, q)
            dve.wait_ge(self_added, H * NB)
            row_out3(0)

            def row_with_stats(m):
                single_lo(m, 0, 0)
                stats_half(m - 1, 0)
                single_lo(m, 0, 1)
                stats_half(m - 1, 1)
                single_lo(m, 0, 2)
                single_lo(m, 0, 3)

            row_with_stats(1)
            row_out3(1)
            with dve.Fori(2, NB) as m:
                row_with_stats(m)
                with dve.Fori(1, m) as i:
                    for q in range(Q):
                        single_lo(m, i, q)
                row_out3(m)
            stats_half(NB - 1, 0)
            stats_half(NB - 1, 1)

            fin = Chain(fin_step, 0)
            dve.wait_ge(o_stats, H * NB)
            dve.wait_ge(turned, 2 * H * NB)
            fin(V.bn_aggr(mv[:, :], ost))
            V.memset(t1[:, P:2 * P], 1.0)
            V.tensor_copy(t1[:, 0:P], mv[:, 0:1].to_broadcast([P, P])).then_inc(fin_cols, 1)
            dve.wait_ge(fin_sum, 1)
            fin(V.tensor_copy(rows[:, :], pC[:, 0:P]))
            V.tensor_scalar_add(deg[:, 0:1], pD[:, 0:1], EPS_PN).then_inc(fin_var, 1)
            dve.wait_ge(fin_root, 1)
            rnorm = deg[:, 1:2]
            fin(V.reciprocal(rnorm, sq[:, 0:1]))
            newton(fin, rnorm, deg[:, 0:1], deg[:, 2:3])
            fin(V.tensor_mul(rnorm, rnorm, deg[:, 2:3]))
            dve.wait_ge(o_stored, H * NB)
            FIRST, PER = fin.count, 2
            NG = N // P
            BG = BLK // P
            MEAN, RSTD, TMP = 6 * NG, 7 * NG, 8 * NG
            with dve.Fori(0, NB) as k:
                step = Chain(fin_step, k * PER + FIRST)
                zk = zr[:, ds(k * BLK, BLK)]
                step(V.tensor_sub(groups(zk), groups(zk), rows[:, :].unsqueeze(1).to_broadcast([P, BG, P])))
                step(V.scalar_tensor_tensor(zk, zk, rnorm, ux[:, ds(k * BLK, BLK)], ALU.mult, ALU.add))
                for j in range(BG):
                    last = V.bn_stats(s1[:, ds((k * BG + j) * 6, 6)], zr[:, ds(k * BLK + j * P, P)])
                last.then_inc(fin_stats, 1)
            dve.wait_ge(fin_stats, NB)
            root = Chain(root_step, 0)
            moments(root, s1[:, 0:6 * NG].rearrange("p (g t) -> p g t", t=6), s1[:, MEAN:MEAN + NG], d[:, :],
                    s1[:, TMP:TMP + NG]).then_inc(fin_var, 1)
            dve.wait_ge(fin_root, 2)
            rstd, tmp = s1[:, RSTD:RSTD + NG], s1[:, TMP:TMP + NG]
            root(V.reciprocal(rstd, rsum[:, :]))
            newton(root, rstd, d[:, :], tmp)
            root(V.tensor_mul(rstd, rstd, tmp))
            with dve.Fori(0, NB) as k:
                for j in range(BG):
                    zg = zr[:, ds(k * BLK + j * P, P)]
                    last = V.tensor_scalar(zg, zg, s1[:, ds(k * BG + j + MEAN, 1)],
                                           s1[:, ds(k * BG + j + RSTD, 1)], ALU.subtract, ALU.mult)
                last.then_inc(fin_norm, 1)

        @block.tensor
        def _(pe):
            T = nc.tensor

            def multiply(n, o, q, layers, sums=False, single=True):
                for j in range(JB):
                    pe.wait_ge(slice_split, n + (o * JB + j + 1))
                    h_, l_ = hi[q % 2 * JB + j], lo[q % 2 * JB + j]
                    end = q == Q - 1 and j == JB - 1
                    for l, banks in layers:
                        p = q // 2 if single else l
                        for stat, moving in ((rhi[q % 2][p], (h_, l_)), (rlo[q % 2][p], (h_,))):
                            for h in range(H):
                                for mov in moving:
                                    last = T.matmul(banks[h][:, :], stat[:, j * P:j * P + P],
                                                    mov[:, h * HALF:(h + 1) * HALF], start=False,
                                                    stop=(end and stat is rlo[q % 2][p]), skip_group_check=True)
                    if sums:
                        for h in range(H):
                            for mov in (h_, l_):
                                last = T.matmul(acc1[h][:, :], onesr[:, :], mov[:, h * HALF:(h + 1) * HALF],
                                                start=False, stop=(end and mov is l_), skip_group_check=True)
                    last.then_inc(slice_multiplied, 1)

            def open_banks(banks):
                for bank in banks:
                    T.matmul(bank[:, 0:2], ident[:, :], zero[:, 0:2], start=True, stop=False,
                             skip_group_check=True)

            def first_product(k, h):
                pe.wait_ge(xT_in, (k * H + h) * 16 + 16)
                for g in range(G):
                    last = T.matmul((pA, pB)[h][:, g * P:g * P + P], t2[:, g * P:g * P + P], w0[:, :],
                                    start=True, stop=True)
                last.then_inc(y_done, 1)

            pe.wait_ge(consts_in, 64)
            pe.wait_ge(ones_set, 1)
            for h in range(H):
                first_product(0, h)

            def pair(k, i):
                for q in range(Q):
                    multiply(n1_pair(k, i), 2 * q, q, [(0, acc0)], sums=True)

            def lower(k, i):
                for q in range(Q):
                    multiply(n1_rest(k, i), q, q, [(0, acc0)], sums=True)

            def row1(k, kind):
                pe.wait_ge(z_ready, k)
                for h in range(H):
                    first_product(k, h)
                pe.wait_ge(banks_free, k - 1)
                open_banks(acc0 + acc1)
                phase1_blocks(pe, k, kind, pair, None, lower)

            pe.wait_ge(setup, 2)
            pe.wait_ge(ident_ready, 1)
            phase1_rows(pe, row1)

            def turn_sum(m, h, first=False):
                g = m * H + h
                pe.wait_ge(t1_filled, g + 1)
                if not first:
                    pe.wait_ge(pA_read, g)
                for j in range(G):
                    last = T.transpose(pA[:, j * P:j * P + P], t1[:, j * P:j * P + P], ident[:, :])
                last.then_inc(turned, 1)

            def turn_x1(m, h, first=False):
                g = m * H + h
                pe.wait_ge(x1_ready, g + 1)
                if not first:
                    pe.wait_ge(x1T_ready, g)
                for j in range(G):
                    last = T.transpose(pB[:, j * P:j * P + P], t1[:, j * P:j * P + P], ident[:, :])
                last.then_inc(x1_turned, 1)

            def make_s1(m, h, first=False):
                g = m * H + h
                pe.wait_ge(x1T_ready, g + 1)
                if not first:
                    pe.wait_ge(s1_ready, g)
                    pe.wait_ge(self_added, g)
                for j in range(G):
                    T.matmul(pC[:, j * P:j * P + P], t2[:, j * P:j * P + P], w1[:, :], start=True, stop=True)
                T.matmul(pD[:, :], wsum[:, :], t2[:, :], start=True, stop=True).then_inc(s1_made, 1)

            def with_update(m, tile, first=False):
                turn_sum(m, 0, first)
                tile(0)
                tile(1)
                turn_x1(m, 0, first)
                tile(2)
                make_s1(m, 0, first)
                turn_sum(m, 1)
                tile(3)
                turn_x1(m, 1)
                make_s1(m, 1)

            L0, L1 = (0, acc0), (1, acc1)

            def diag(m, q):
                multiply(n2(m, 0), q, q, [L0], single=False)

            def dual(m, i, q):
                multiply(n2(m, i), q, q, [L0, L1], single=False)

            pe.wait_ge(banks_free, NB - 1)
            open_banks(acc0)
            for q in range(Q):
                diag(0, q)
            pe.wait_ge(banks_free, row2(0))
            open_banks(acc0 + acc1)
            with_update(0, lambda q: diag(1, q), first=True)
            for q in range(Q):
                dual(1, 1, q)
            with pe.Fori(2, NB) as m:
                pe.wait_ge(banks_free, row2(m - 1))
                open_banks(acc0 + acc1)
                for q in range(Q):
                    diag(m, q)
                with_update(m - 1, lambda q: dual(m, 1, q))
                with pe.Fori(2, m + 1) as i:
                    for q in range(Q):
                        dual(m, i, q)

            L3 = (1, acc0)

            def single(m, i, q, single=True):
                multiply(n3(m, i), q, q, [L3], single=single)

            def turn_o(m, h, first=False):
                g = m * H + h
                pe.wait_ge(t1_filled, g + (H * NB + 1))
                if first:
                    pe.wait_ge(pA_read, H * NB)
                else:
                    pe.wait_ge(o_stored, g)
                for j in range(G):
                    last = T.transpose(pA[:, j * P:j * P + P], t1[:, j * P:j * P + P], ident[:, :])
                last.then_inc(turned, 1)

            def row_with_turn(m, first=False):
                single(m, 0, 0)
                turn_o(m - 1, 0, first)
                single(m, 0, 1)
                turn_o(m - 1, 1)
                single(m, 0, 2)
                single(m, 0, 3)

            pe.wait_ge(banks_free, row2(NB - 1))
            open_banks(acc0)
            with_update(NB - 1, lambda q: single(0, 0, q, single=False))
            with pe.Fori(1, NB) as i:
                for q in range(Q):
                    single(0, i, q)
            pe.wait_ge(banks_free, row3(0))
            open_banks(acc0)
            row_with_turn(1, first=True)
            with pe.Fori(2, NB) as m:
                pe.wait_ge(banks_free, row3(m - 1))
                open_banks(acc0)
                row_with_turn(m)
                with pe.Fori(1, m) as i:
                    for q in range(Q):
                        single(m, i, q)
            for h in range(H):
                turn_o(NB - 1, h)

            pe.wait_ge(fin_cols, 1)
            T.matmul(pC[:, 0:P], t1[:, 0:P], ident[:, :], start=True, stop=True)
            T.matmul(pD[:, 0:1], t1[:, P:2 * P], mv[:, 1:2], start=True, stop=True).then_inc(fin_sum, 1)


def kernel(x, adj, L0_gnn_W, L0_gnn_b, L1_gnn_weight, L1_gnn_self_weight):
    import numpy as np
    import concourse.bacc as bacc
    from concourse.bass_utils import run_bass_kernel_spmd

    x, adj = np.asarray(x), np.asarray(adj)
    n, f = x.shape
    nb, q, jb = n // 1024, 4, 2
    blocks = adj.reshape(nb, 1024, nb, 1024)
    adj_t = np.ascontiguousarray(
        blocks.reshape(nb, 1024, nb, q, jb, 128).transpose(0, 2, 3, 5, 4, 1)).reshape(nb, nb, q, 128, jb * 1024)
    adj_n = np.ascontiguousarray(
        blocks.reshape(nb, q, jb, 128, nb, 1024).transpose(0, 4, 1, 3, 2, 5)).reshape(nb, nb, q, 128, jb * 1024)
    arrays = {
        "x": np.ascontiguousarray(x),
        "xT": np.ascontiguousarray(x.T),
        "adjT": adj_t,
        "adjN": adj_n,
        "W0": np.ascontiguousarray(L0_gnn_W),
        "b_rows": np.ascontiguousarray(np.broadcast_to(np.asarray(L0_gnn_b)[None, :], (128, f))),
        "W1": np.ascontiguousarray(L1_gnn_weight),
        "Wself": np.ascontiguousarray(L1_gnn_self_weight),
    }
    nc = bacc.Bacc("TRN2", target_bir_lowering=False, num_devices=1)
    f32 = mybir.dt.float32
    args = [nc.dram_tensor(f"in_{name}", a.shape, f32, kind="ExternalInput").ap() for name, a in arrays.items()]
    out = nc.dram_tensor("out", (n, f), f32, kind="ExternalOutput").ap()
    graph_kernel(nc, *args, out)
    r = run_bass_kernel_spmd(nc, [{f"in_{name}": a for name, a in arrays.items()}], core_ids=[0])
    return r.results[0]["out"]
```

```python
import concourse.bass as bass
from concourse import mybir
from contextlib import ExitStack


def graph_kernel(nc, x, xT, adjT, adjN, W0, b_rows, W1, Wself, out):
    f32 = mybir.dt.float32
    f32r = mybir.dt.float32r
    ACT = mybir.ActivationFunctionType
    ALU = mybir.AluOpType
    AX = mybir.AxisListType
    ds = bass.ds

    P = 128
    N = x.shape[0]
    F = x.shape[1]
    assert F == P
    BLK = 1024
    NB = N // BLK
    Q = 4
    JB = BLK // Q // P
    TILE = JB * BLK
    H = BLK // 512
    HALF = 512
    G = HALF // P
    EPS_LN = 1e-5
    EPS_PN = 1e-6
    assert NB >= 8 and NB % 2 == 0 and JB == 2 and H == 2

    S = Q * JB
    LOWER = NB * (NB - 1) // 2
    UPPER = NB * (NB + 1) // 2
    N2 = NB * NB * S
    N3 = N2 + UPPER * S
    SKIP = N2 - (LOWER + 1) * S

    def n1(k, c):
        return k * (NB * S) + c * S

    def n1_pair(k, i):
        return k * (NB * S) + i * (2 * S)

    def n1_rest(k, i):
        return k * ((NB - 2) * S) + i * S + 2 * NB * S

    def u1(k, c):
        return (k * (k - 1)) * (S // 2) + c * S + S

    def u1_rest(k, i):
        return (k * (k - 3)) * (S // 2) + i * S + (NB + 1) * S

    def within(v):
        return v if isinstance(v, int) else v.with_bounds(min_val=0, max_val=NB - 1)

    def phase1_rows(eng, row):
        row(1, "first")
        with eng.Fori(2, NB // 2) as k:
            row(k, "few")
        row(NB // 2, "half")
        with eng.Fori(NB // 2 + 1, NB - 1) as k:
            row(k, "many")
        row(NB - 1, "last")

    def phase1_blocks(eng, k, kind, first_pair, pair, natural, lower, after_lower=None):
        first_pair(k)
        if kind in ("few", "half", "many"):
            with eng.Fori(1, {"few": k, "half": NB // 2, "many": k * -1 + NB}[kind]) as i:
                pair(k, i)
        if kind in ("first", "few") and natural:
            with eng.Fori(k * 2, NB) as c:
                natural(k, c)
        if kind in ("many", "last"):
            with eng.Fori(0, k * 2 - NB) as i:
                lower(k, i)
            if after_lower:
                after_lower()

    def summed_on_dve(q, j):
        return j == 0 and q < Q - 1

    def n2(m, i):
        return (m * (m + 1)) * (S // 2) + i * S + N2

    def n3(m, i):
        return i * S + N3 if isinstance(m, int) and m == 0 else (m * (m - 1)) * (S // 2) + i * S + (N3 + NB * S)

    def no_tile(q):
        pass

    def k2(m):
        return m * -1 + (NB - 1)

    def row2(m):
        return m + NB

    def row3(m):
        return m + 2 * NB

    def k3(m):
        return NB - 1 if isinstance(m, int) and m == 0 else m - 1

    def col3(m, i):
        return i * -1 + (NB - 1) if isinstance(m, int) and m == 0 else i

    ctx = ExitStack()
    with ctx:
        def sb(name, shape, dt=f32):
            return ctx.enter_context(nc.sbuf_tensor(name, shape, dt))

        def pb(name):
            return ctx.enter_context(nc.psum_tensor(name, [P, HALF], f32))

        def sem(name):
            return ctx.enter_context(nc.semaphore(name))

        zr = sb("zr", [P, NB * BLK])
        s1 = sb("s1", [P, NB * BLK])
        ux = sb("ux", [P, NB * BLK])
        o1 = sb("o1", [P, NB * BLK])

        raw = [sb(f"raw{q}", [P, TILE]) for q in range(Q)]
        hi = [sb(f"hi{r}", [P, BLK], f32r) for r in range(2 * JB)]
        lo = [sb(f"lo{r}", [P, BLK], f32r) for r in range(2 * JB)]
        rhi = [[sb(f"rhi{r}{l}", [P, JB * P], f32r) for l in range(2)] for r in range(2)]
        rlo = [[sb(f"rlo{r}{l}", [P, JB * P], f32r) for l in range(2)] for r in range(2)]

        t1 = sb("t1", [P, HALF])
        t2 = sb("t2", [P, HALF])
        w0 = sb("w0", [P, P])
        w1 = sb("w1", [P, P])
        wsum = sb("wsum", [P, P])
        ident = sb("ident", [P, P])
        rows = sb("rows", [P, P])
        d = sb("d", [P, N // P])
        rsum = sb("rsum", [P, NB * BLK // P])
        deg = sb("deg", [P, BLK // P])
        sq = sb("sq", [P, BLK // P])
        nw = sb("nw", [P, BLK // P])
        low = sb("low", [P, BLK // P])
        onesr = sb("onesr", [P, P], f32r)
        st = sb("st", [P, G, 6])
        ost = w0[:, 0:H * NB * 6]
        mean = sb("mean", [P, G])
        mv = sb("mv", [P, 2])
        zero = sb("zero", [P, BLK // P])
        xT_blk = o1[:, BLK:2 * BLK]
        colsum = o1[:, 0:BLK]
        pn_scale = deg[:, 1:2]
        pn_bias = deg[:, 2:3]
        BG = BLK // P
        MEAN, RSTD, TMP, BIAS = (f * (N // P) for f in (6, 7, 8, 9))
        BATCH = NB // 2
        NACT = BATCH + 1

        acc0 = [pb(f"acc0{h}") for h in range(H)]
        acc1 = [pb(f"acc1{h}") for h in range(H)]
        pA = pb("pA")
        pB = pb("pB")
        pC = pb("pC")
        pD = pb("pD")

        loaded = [sem(f"loaded{q}") for q in range(Q)]
        consts_in = sem("consts_in")
        ident_zero = sem("ident_zero")
        ident_ready = sem("ident_ready")
        ones_set = sem("ones_set")
        setup = sem("setup")
        hi_ready = sem("hi_ready")
        slice_split = sem("slice_split")
        slice_multiplied = sem("slice_multiplied")
        banks_free = sem("banks_free")
        xT_in = sem("xT_in")
        y_done = sem("y_done")
        z_ready = sem("z_ready")
        deg_ready = sem("deg_ready")
        deg_root = sem("deg_root")
        deg_step = sem("deg_step")
        low_step = sem("low_step")
        low_ready = sem("low_ready")
        colsum_used = sem("colsum_used")
        x_in = sem("x_in")
        acc0_read = sem("acc0_read")
        half_summed = sem("half_summed")
        acc1_read = sem("acc1_read")
        turned = sem("turned")
        upd_step = sem("upd_step")
        var_ready = sem("var_ready")
        var_root = sem("var_root")
        x1_ready = sem("x1_ready")
        x1_stored = sem("x1_stored")
        x1_turned = sem("x1_turned")
        x1T_ready = sem("x1T_ready")
        s1_made = sem("s1_made")
        s1_ready = sem("s1_ready")
        self_added = sem("self_added")
        o_ready = sem("o_ready")
        o_stats = sem("o_stats")
        fin_step = sem("fin_step")
        fin_sum = sem("fin_sum")
        fin_stats = sem("fin_stats")
        root_step = sem("root_step")
        fin_root = sem("fin_root")
        fin_var = sem("fin_var")
        pn_ready = sem("pn_ready")
        o_normed = sem("o_normed")
        o_turned = sem("o_turned")
        o_added = sem("o_added")
        sum_stats = sem("sum_stats")
        ln_ready = sem("ln_ready")
        act_normed = sem("act_normed")
        dve_normed = sem("dve_normed")
        out_done = sem("out_done")

        block = ctx.enter_context(nc.Block())

        def half(t, k, h):
            return t[:, ds(k * BLK + h * HALF, HALF)]

        def groups(ap):
            return ap.rearrange("p (g f) -> p g f", f=P)

        @block.sync
        def _(sp):
            def load_tile(src, k, c, q, n, o, first=False):
                if not first:
                    sp.wait_ge(slice_split, n + (o + 1 - Q) * JB)
                sp.dma_start(raw[o % Q][:, :], src[k, c, q]).then_inc(loaded[o % Q], 16)

            def load_block(src, k, c, n, first=False):
                for q in range(Q):
                    load_tile(src, k, c, q, n, q, first)

            def load_pair(k, i):
                for q in range(Q):
                    load_tile(adjT, k, i, q, n1_pair(k, i), 2 * q)
                    load_tile(adjN, k, within(k + i), q, n1_pair(k, i), 2 * q + 1)

            load_block(adjN, 0, 0, 0, first=True)
            with sp.Fori(1, NB) as c:
                load_block(adjN, 0, c, n1(0, c))
            phase1_rows(sp, lambda k, kind: phase1_blocks(
                sp, k, kind, lambda k: load_pair(k, 0), load_pair,
                lambda k, c: load_block(adjN, k, c, n1(k, c)),
                lambda k, i: load_block(adjT, k, within(i + (k * -1 + NB)), n1_rest(k, i))))
            load_block(adjT, NB - 1, NB - 1, N2)
            with sp.Fori(1, NB) as m:
                load_block(adjT, k2(m), k2(m), n2(m, 0))
                with sp.Fori(1, m + 1) as i:
                    load_block(adjT, k2(m), i * -1 + NB, n2(m, i))
            with sp.Fori(0, NB) as i:
                load_block(adjT, NB - 1, col3(0, i), n3(0, i))
            with sp.Fori(1, NB) as m:
                with sp.Fori(0, m) as i:
                    load_block(adjT, k3(m), i, n3(m, i))

        @block.gpsimd
        def _(pool):
            pool.dma_start(w0[:, :], W0).then_inc(consts_in, 16)
            pool.dma_start(w1[:, :], W1).then_inc(consts_in, 16)
            pool.dma_start(t1[:, 0:P], Wself).then_inc(consts_in, 16)
            pool.dma_start(rows[:, :], b_rows).then_inc(consts_in, 16)
            pool.dma_start(xT_blk, xT[:, 0:BLK]).then_inc(xT_in, 16)
            pool.memset(ident[:, :], 0.0).then_inc(ident_zero, 1)
            pool.wait_ge(ident_zero, 1)
            pool.affine_select(out=ident[:, :], in_=ident[:, :], compare_op=ALU.not_equal, fill=1.0,
                               base=0, pattern=[[-1, P]], channel_multiplier=1).then_inc(ident_ready, 1)
            def load_x(k):
                pool.dma_start(groups(s1[:, ds(k * BLK, BLK)]),
                               x[ds(k * BLK, BLK), :].rearrange("(g p) f -> p g f", p=P)).then_inc(x_in, 16)

            with pool.Fori(1, NB) as k:
                pool.wait_ge(y_done, k * H)
                pool.dma_start(xT_blk, xT[:, ds(k * BLK, BLK)]).then_inc(xT_in, 16)
            pool.wait_ge(y_done, H * NB)
            with pool.Fori(0, NB) as k:
                load_x(k)

            def store(k):
                pool.dma_start(out[ds(k * BLK, BLK), :].rearrange("(g p) f -> p g f", p=P),
                               groups(zr[:, ds(k * BLK, BLK)])).then_inc(out_done, 16)

            def store_act(k):
                pool.wait_ge(act_normed, k + 1)
                store(k)

            def store_dve(i):
                pool.wait_ge(dve_normed, i + 1)
                store(i + NACT)

            with pool.Fori(0, NACT - 1) as k:
                store_act(k)
            with pool.Fori(0, NB - NACT - 1) as i:
                store_dve(i)
            store_act(NACT - 1)
            store_dve(NB - NACT - 1)
            pool.wait_ge(out_done, 16 * NB)

        @block.scalar
        def _(act):
            def split_hi(n, o, u, c, q, layers, rows_known, single=True):
                act.wait_ge(slice_multiplied, u + (q * JB - 3 * JB if single else q * JB - JB))
                if rows_known is not None:
                    act.wait_ge(*rows_known)
                for l in layers:
                    src = (zr, s1)[l]
                    nc.scalar.activation(rhi[q % 2][q // 2 if single else l][:, :],
                                         src[:, ds(c * BLK + q * JB * P, JB * P)], ACT.Copy)
                act.wait_ge(loaded[o % Q], n * (16 // S) + 16 * (o // Q + 1))
                for j in range(JB):
                    act.wait_ge(slice_multiplied, u + (q - 2) * JB + (j + 1))
                    nc.scalar.activation(hi[q % 2 * JB + j][:, :], raw[o % Q][:, j * BLK:(j + 1) * BLK],
                                         ACT.Copy).then_inc(hi_ready, 1)

            def degree_root(k):
                act.wait_ge(deg_ready, k + 1)
                nc.scalar.activation(sq[:, :], deg[:, :], ACT.Sqrt).then_inc(deg_root, 1)

            def lower_hi(k, i):
                for q in range(Q):
                    split_hi(n1_rest(k, i), q, u1_rest(k, i), within(i + (k * -1 + NB)), q, [0], (z_ready, k))

            def pair_hi(k, i):
                for q in range(Q):
                    split_hi(n1_pair(k, i), 2 * q, u1(k, i), i, q, [0], (z_ready, i + 1))

            def copy_acc0(k):
                act.wait_ge(slice_multiplied, u1(k + 1, 0))
                for h in range(H):
                    ins = nc.scalar.activation(half(ux, k, h), acc0[h][:, :], ACT.Copy)
                ins.then_inc(acc0_read, 1)

            def first_pair_hi(k, start):
                for q in range(Q):
                    split_hi(n1_pair(k, 0), 2 * q, u1(k, 0), 0, q, [0], (z_ready, 1) if start else None)
                    if q == 0 and not start:
                        copy_acc0(k - 1)
                    if q == 1 and not start:
                        degree_root(k - 1)

            def row1(k, kind):
                phase1_blocks(act, k, kind, lambda k: first_pair_hi(k, kind == "first"), pair_hi, None, lower_hi)

            degree_root(0)
            phase1_rows(act, row1)
            copy_acc0(NB - 1)
            degree_root(NB - 1)

            def row_out2(m, dual=True):
                act.wait_ge(slice_multiplied, n2(m + 1, 0) - SKIP)
                nc.scalar.activation(t2[:, :], acc0[1][:, :], ACT.Copy).then_inc(acc0_read, 1)
                if dual:
                    for h in range(H):
                        ins = nc.scalar.activation(half(o1, k2(m), h), acc1[h][:, :], ACT.Copy)
                    ins.then_inc(acc1_read, 1)

            def root_var(m, h):
                g = m * H + h
                act.wait_ge(var_ready, g + 1)
                nc.scalar.activation(sq[:, 0:G], nw[:, 0:G], ACT.Sqrt).then_inc(var_root, 1)

            def copy_x1T(m, h, first=False):
                g = m * H + h
                act.wait_ge(x1_turned, g + 1)
                if not first:
                    act.wait_ge(s1_made, g)
                nc.scalar.activation(t2[:, :], pC[:, :], ACT.Copy).then_inc(x1T_ready, 1)
                nc.scalar.activation(half(ux, k2(m), h), t1[:, :], ACT.Copy).then_inc(x1_stored, 1)

            def copy_s1(m, h):
                g = m * H + h
                act.wait_ge(s1_made, g + 1)
                nc.scalar.activation(half(s1, k2(m), h), pC[:, :], ACT.Copy).then_inc(s1_ready, 1)

            for q in range(Q):
                split_hi(N2, q, N2 - SKIP, NB - 1, q, [0], (z_ready, NB), single=False)

            def diag_hi(m, q):
                split_hi(n2(m, 0), q, n2(m, 0) - SKIP, k2(m), q, [0], None, single=False)

            def dual_hi(m, i, q):
                split_hi(n2(m, i), q, n2(m, i) - SKIP, i * -1 + NB, q, [0, 1],
                         (s1_ready, i * H + (q // (Q // H) - 1)), single=False)

            def with_update(m, first, second, third, dual=True, start=False):
                first(0)
                row_out2(m, dual)
                first(1)
                first(2)
                first(3)
                second(0)
                second(1)
                root_var(m, 0)
                second(2)
                second(3)
                copy_x1T(m, 0, start)
                root_var(m, 1)
                copy_s1(m, 0)
                third(0)
                third(1)
                copy_x1T(m, 1)
                copy_s1(m, 1)
                third(2)
                third(3)

            def with_late_update(m, first, second, third):
                first(0)
                row_out2(m)
                for q in range(1, Q):
                    first(q)
                second(0)
                second(1)
                second(2)
                root_var(m, 0)
                second(3)
                third(0)
                copy_x1T(m, 0)
                third(1)
                root_var(m, 1)
                copy_s1(m, 0)
                third(2)
                third(3)
                copy_x1T(m, 1)
                copy_s1(m, 1)

            with_update(0, lambda q: diag_hi(1, q), no_tile, lambda q: dual_hi(1, 1, q), dual=False, start=True)
            with_update(1, lambda q: diag_hi(2, q), lambda q: dual_hi(2, 1, q), lambda q: dual_hi(2, 2, q))
            with act.Fori(3, NB) as m:
                with_late_update(m - 1, lambda q: diag_hi(m, q), lambda q: dual_hi(m, 1, q), lambda q: dual_hi(m, 2, q))
                with act.Fori(3, m + 1) as i:
                    for q in range(Q):
                        dual_hi(m, i, q)

            def single_hi(m, i, q, single=True):
                first_row = isinstance(m, int) and m == 0
                split_hi(n3(m, i), q, n3(m, i) - SKIP, col3(m, i), q, [1],
                         (s1_ready, i * H + H) if first_row else None, single)

            def relu_o(m):
                act.wait_ge(banks_free, row3(m))
                for h in range(H):
                    nc.scalar.activation(half(o1, k3(m), h), half(o1, k3(m), h), ACT.Relu).then_inc(o_ready, 1)

            with_late_update(NB - 1, lambda q: single_hi(0, 0, q, single=False), lambda q: single_hi(0, 1, q),
                        lambda q: single_hi(0, 2, q))
            with act.Fori(3, NB) as i:
                for q in range(Q):
                    single_hi(0, i, q)

            def row_with_relu(m):
                single_hi(m, 0, 0)
                single_hi(m, 0, 1)
                relu_o(m - 1)
                single_hi(m, 0, 2)
                single_hi(m, 0, 3)

            row_with_relu(1)
            with act.Fori(2, NB) as m:
                row_with_relu(m)
                with act.Fori(1, m) as i:
                    for q in range(Q):
                        single_hi(m, i, q)
            relu_o(NB - 1)

            act.wait_ge(fin_var, 1)
            nc.scalar.activation(sq[:, 0:1], deg[:, 0:1], ACT.Sqrt).then_inc(fin_root, 1)
            act.wait_ge(pn_ready, 1)

            def pair_norm(k, first=False):
                for h in range(H):
                    if not first:
                        act.wait_ge(o_turned, k * H + (h - 1))
                    nc.scalar.activation((t1, t2)[h][:, :], half(o1, k, h), ACT.Identity,
                                         bias=pn_bias, scale=pn_scale).then_inc(o_normed, 1)

            def norm_groups(k, js):
                for j in js:
                    zg = zr[:, ds(k * BLK + j * P, P)]
                    ins = nc.scalar.activation(zg, zg, ACT.Identity, bias=s1[:, ds(k * BG + (j + BIAS), 1)],
                                               scale=s1[:, ds(k * BG + (j + RSTD), 1)])
                return ins

            def last_norm(k):
                norm_groups(k, range(BG)).then_inc(act_normed, 1)

            def last_root(b):
                act.wait_ge(fin_var, b + 2)
                nc.scalar.activation(rsum[:, b * BATCH * BG:(b + 1) * BATCH * BG],
                                     d[:, b * BATCH * BG:(b + 1) * BATCH * BG], ACT.Sqrt).then_inc(fin_root, 1)

            pair_norm(0, first=True)
            with act.Fori(1, BATCH) as k:
                pair_norm(k)
            pair_norm(BATCH)
            last_root(0)
            pair_norm(BATCH + 1)
            act.wait_ge(ln_ready, 1)
            with act.Fori(BATCH + 2, NB - 1) as k:
                pair_norm(k)
            norm_groups(0, range(G))
            pair_norm(NB - 1)
            norm_groups(0, range(G, BG)).then_inc(act_normed, 1)
            last_norm(1)
            last_root(1)
            with act.Fori(2, BATCH) as k:
                last_norm(k)
            act.wait_ge(ln_ready, 2)
            last_norm(BATCH)

        @block.vector
        def _(dve):
            V = nc.vector

            class Chain:

                def __init__(self, s, base):
                    self.s, self.base, self.count = s, base, 0

                def __call__(self, ins):
                    self.count += 1
                    ins.then_inc(self.s, 1)
                    dve.wait_ge(self.s, self.base + self.count)

            V.memset(o1[:, (NB - 1) * BLK:NB * BLK], 0.0)
            V.memset(ux[:, 0:BLK], 0.0).then_inc(colsum_used, 1)
            V.memset(onesr[:, :].bitcast(f32), 1.0).then_inc(ones_set, 1)
            V.memset(zero[:, :], 0.0).then_inc(slice_multiplied, S)
            V.memset(rsum[:, :], 0.0).then_inc(setup, 1)
            dve.wait_ge(consts_in, 64)
            V.tensor_add(wsum[:, :], w1[:, :], t1[:, 0:P]).then_inc(setup, 1)
            dve.wait_ge(setup, 2)
            dve.wait_ge(ident_ready, 1)

            def split_lo(n, o, u, c, q, layers, single=True):
                for j in range(JB):
                    dve.wait_ge(hi_ready, u + (q * JB + j + 1 - S))
                    if j == 0:
                        for l in layers:
                            src, p = (zr, s1)[l], q // 2 if single else l
                            V.tensor_sub(rlo[q % 2][p][:, :], src[:, ds(c * BLK + q * JB * P, JB * P)],
                                         rhi[q % 2][p][:, :].bitcast(f32))
                    r = q % 2 * JB + j
                    V.tensor_sub(lo[r][:, :], raw[o % Q][:, j * BLK:(j + 1) * BLK],
                                 hi[r][:, :].bitcast(f32)).then_inc(slice_split, 1)

            def sum_tile(c, q, n, o):
                dve.wait_ge(loaded[o % Q], n * (16 // S) + 16 * (o // Q + 1))
                V.tensor_reduce(rsum[:, ds(c * (BLK // P) + q * JB, JB)],
                                raw[o % Q][:, :].rearrange("p (g j) -> p g j", g=JB),
                                AX.X, ALU.add).then_inc(slice_split, JB)

            def sum_rows(k, c):
                for q in range(Q):
                    sum_tile(c, q, n1(k, c), q)

            DEG_STEPS = 7

            def newton(step, r, v, tmp):
                step(V.tensor_mul(tmp, r, r))
                step(V.tensor_mul(tmp, tmp, v))
                step(V.tensor_scalar(tmp, tmp, -0.5, 1.5, ALU.mult, ALU.add))

            def own_sums(k, step):
                dve.wait_ge(slice_split, k * (NB * S) + NB * S)
                step(V.tensor_reduce(deg[:, :], rsum[:, :].rearrange("p (c g) -> p g c", c=NB), AX.X, ALU.add))

            def degree(k, step, lower):
                if lower:
                    dve.wait_ge(low_ready, k)
                    step(V.scalar_tensor_tensor(deg[:, :], deg[:, :], 1.0, low[:, :], ALU.add, ALU.add))
                else:
                    step(V.tensor_scalar_add(deg[:, :], deg[:, :], 1.0))
                V.tensor_copy(rsum[:, ds(k * (BLK // P), BLK // P)], zero[:, :]).then_inc(deg_ready, 1)

            def make_z(k, step):
                dve.wait_ge(deg_root, k + 1)
                dk = d[:, ds(k * (BLK // P), BLK // P)]
                step(V.reciprocal(dk, sq[:, :]))
                newton(step, dk, deg[:, :], nw[:, :])
                step(V.tensor_mul(dk, dk, nw[:, :]))
                for h in range(H):
                    dve.wait_ge(y_done, k * H + (h + 1))
                    last = V.tensor_mul(groups(half(zr, k, h)), groups((pA, pB)[h][:, :]),
                                        d[:, ds(k * (BLK // P) + h * G, G)].unsqueeze(2).to_broadcast([P, G, P]))
                last.then_inc(z_ready, 1)
                assert step.count == DEG_STEPS

            def lower_sums(k):
                step = Chain(low_step, (k - 1) * (2 * H - 2))
                dve.wait_ge(slice_multiplied, u1(k + 1, 0))
                for h in range(H):
                    ins = V.tensor_mul(groups(t1[:, :]), groups(acc1[h][:, :]),
                                       ident[:, :].unsqueeze(1).to_broadcast([P, G, P]))
                    if h == H - 1:
                        ins.then_inc(banks_free, 1)
                        dve.wait_ge(banks_free, k)
                    else:
                        step(ins)
                    ins = V.tensor_reduce(low[:, h * G:h * G + G], groups(t1[:, :]), AX.X, ALU.add)
                    if h == H - 1:
                        ins.then_inc(low_ready, 1)
                    else:
                        step(ins)

            sum_rows(0, 0)
            with dve.Fori(1, NB) as c:
                sum_rows(0, c)
            step = Chain(deg_step, 0)
            own_sums(0, step)
            degree(0, step, lower=False)
            make_z(0, step)

            def lo_of_pair(k, i, q):
                split_lo(n1_pair(k, i), 2 * q, u1(k, i), i, q, [0])

            def sum_of_pair(k, i, q):
                sum_tile(within(k + i), q, n1_pair(k, i), 2 * q + 1)

            def pair_lo(k, i):
                for q in range(Q):
                    lo_of_pair(k, i, q)
                    sum_of_pair(k, i, q)

            def lower_lo(k, i):
                for q in range(Q):
                    n = n1_rest(k, i)
                    for j in range(JB):
                        if summed_on_dve(q, j):
                            dve.wait_ge(loaded[q], n * (16 // S) + 16)
                            dve.wait_ge(slice_split, n + q * JB)
                            V.tensor_add(colsum, colsum, raw[q][:, j * BLK:(j + 1) * BLK])
                    split_lo(n1_rest(k, i), q, u1_rest(k, i), within(i + (k * -1 + NB)), q, [0])

            def first_pair_lo(k, kind):
                step = Chain(deg_step, (k - 1) * DEG_STEPS)
                own_sums(k - 1, step)
                lo_of_pair(k, 0, 0)
                if kind in ("many", "last"):
                    dve.wait_ge(colsum_used, k - NB // 2)
                lower_sums(k - 1)
                if kind in ("many", "last"):
                    V.memset(colsum, 0.0)
                sum_of_pair(k, 0, 0)
                lo_of_pair(k, 0, 1)
                degree(k - 1, step, lower=True)
                sum_of_pair(k, 0, 1)
                lo_of_pair(k, 0, 2)
                sum_of_pair(k, 0, 2)
                make_z(k - 1, step)
                lo_of_pair(k, 0, 3)
                sum_of_pair(k, 0, 3)

            def row1(k, kind):
                first = (lambda k: pair_lo(k, 0)) if kind == "first" else (lambda k: first_pair_lo(k, kind))
                phase1_blocks(dve, k, kind, first, pair_lo, sum_rows, lower_lo)

            phase1_rows(dve, row1)
            step = Chain(deg_step, (NB - 1) * DEG_STEPS)
            own_sums(NB - 1, step)
            dve.wait_ge(colsum_used, NB // 2)
            lower_sums(NB - 1)
            degree(NB - 1, step, lower=True)
            make_z(NB - 1, step)

            def moments(step, six, mean, var, tmp):
                V.tensor_add(mean, six[:, :, 1], six[:, :, 4])
                V.tensor_sub(tmp, six[:, :, 1], six[:, :, 4])
                step(V.tensor_add(var, six[:, :, 2], six[:, :, 5]))
                V.tensor_scalar_mul(mean, mean, 0.5)
                V.scalar_tensor_tensor(tmp, tmp, 0.25, tmp, ALU.mult, ALU.mult)
                step(V.tensor_scalar(var, var, 1.0 / P, EPS_LN, ALU.mult, ALU.add))
                return V.tensor_add(var, var, tmp)

            SUM_STEPS, STATS_STEPS, ROOT_STEPS = 4, 3, 5
            UPD_STEPS = SUM_STEPS + STATS_STEPS + ROOT_STEPS

            def update_sum(m, h):
                g = m * H + h
                k = k2(m)
                p = (pA, pB)[h][:, :]
                step = Chain(upd_step, g * UPD_STEPS)
                dve.wait_ge(turned, g + 1)
                step(V.tensor_add(p, p, half(zr, k, h)))
                step(V.tensor_mul(groups(p), groups(p),
                                  d[:, ds(k * (BLK // P) + h * G, G)].unsqueeze(2).to_broadcast([P, G, P])))
                step(V.tensor_add(groups(p), groups(p), rows[:, :].unsqueeze(1).to_broadcast([P, G, P])))
                step(V.scalar_tensor_tensor(p, p, 0.0, half(s1, k, h), ALU.max, ALU.add))
                assert step.count == SUM_STEPS, step.count

            def update_stats(m, h):
                g = m * H + h
                p = (pA, pB)[h][:, :]
                step = Chain(upd_step, g * UPD_STEPS + SUM_STEPS)
                for j in range(G):
                    last = V.bn_stats(st[:, j, :], p[:, j * P:j * P + P])
                step(last)
                moments(step, st[:, :, :], mean[:, :], nw[:, 0:G], deg[:, G:2 * G]).then_inc(var_ready, 1)
                assert step.count == STATS_STEPS, step.count

            def update_norm(m, h):
                g = m * H + h
                p = (pA, pB)[h][:, :]
                step = Chain(upd_step, g * UPD_STEPS + (SUM_STEPS + STATS_STEPS))
                dve.wait_ge(var_root, g + 1)
                step(V.reciprocal(deg[:, 0:G], sq[:, 0:G]))
                newton(step, deg[:, 0:G], nw[:, 0:G], deg[:, G:2 * G])
                step(V.tensor_mul(deg[:, 0:G], deg[:, 0:G], deg[:, G:2 * G]))
                if h == 1:
                    dve.wait_ge(x1_stored, g)
                for j in range(G):
                    last = V.tensor_scalar(t1[:, j * P:j * P + P], p[:, j * P:j * P + P], mean[:, j:j + 1],
                                           deg[:, j:j + 1], ALU.subtract, ALU.mult)
                last.then_inc(x1_ready, 1)
                assert step.count == ROOT_STEPS, step.count

            def add_self(m, h):
                g = m * H + h
                k = k2(m)
                dve.wait_ge(s1_made, g + 1)
                V.tensor_add(half(o1, k, h), half(o1, k, h), pD[:, :]).then_inc(self_added, 1)

            def row_out2(m, start):
                k = k2(m)
                dve.wait_ge(slice_multiplied, n2(m + 1, 0) - SKIP)
                if not start:
                    dve.wait_ge(x1_stored, m * H)
                V.tensor_add(t1[:, :], half(ux, k, 0), acc0[0][:, :]).then_inc(banks_free, 1)
                dve.wait_ge(acc0_read, m + NB)
                V.tensor_add(t2[:, :], half(ux, k, 1), t2[:, :]).then_inc(half_summed, 1)

            def diag_lo(m, q):
                split_lo(n2(m, 0), q, n2(m, 0) - SKIP, k2(m), q, [0], single=False)

            def dual_lo(m, i, q):
                split_lo(n2(m, i), q, n2(m, i) - SKIP, i * -1 + NB, q, [0, 1], single=False)

            for q in range(Q):
                split_lo(N2, q, N2 - SKIP, NB - 1, q, [0], single=False)

            def with_update(m, first, second, third, start=False):
                first(0)
                row_out2(m, start)
                first(1)
                first(2)
                first(3)
                second(0)
                update_sum(m, 0)
                update_stats(m, 0)
                second(1)
                update_norm(m, 0)
                second(2)
                update_sum(m, 1)
                update_stats(m, 1)
                second(3)
                update_norm(m, 1)
                add_self(m, 0)
                third(0)
                third(1)
                add_self(m, 1)
                third(2)
                third(3)

            def with_late_update(m, first, second, third):
                first(0)
                row_out2(m, False)
                for q in range(1, Q):
                    first(q)
                second(0)
                second(1)
                update_sum(m, 0)
                update_stats(m, 0)
                second(2)
                update_norm(m, 0)
                second(3)
                update_sum(m, 1)
                third(0)
                update_stats(m, 1)
                third(1)
                update_norm(m, 1)
                add_self(m, 0)
                third(2)
                third(3)
                add_self(m, 1)

            dve.wait_ge(x_in, NB * 16)
            with_update(0, lambda q: diag_lo(1, q), no_tile, lambda q: dual_lo(1, 1, q), start=True)
            with_update(1, lambda q: diag_lo(2, q), lambda q: dual_lo(2, 1, q), lambda q: dual_lo(2, 2, q))
            with dve.Fori(3, NB) as m:
                with_late_update(m - 1, lambda q: diag_lo(m, q), lambda q: dual_lo(m, 1, q), lambda q: dual_lo(m, 2, q))
                with dve.Fori(3, m + 1) as i:
                    for q in range(Q):
                        dual_lo(m, i, q)

            def single_lo(m, i, q, single=True):
                split_lo(n3(m, i), q, n3(m, i) - SKIP, col3(m, i), q, [1], single)

            def row_out3(m):
                k = k3(m)
                dve.wait_ge(slice_multiplied, n3(m + 1, 0) - SKIP)
                for h in range(H):
                    last = V.tensor_add(half(o1, k, h), half(o1, k, h), acc0[h][:, :])
                last.then_inc(banks_free, 1)

            def stats_o(m):
                for h in range(H):
                    g = m * H + h
                    dve.wait_ge(o_ready, g + 1)
                    V.bn_stats(w0[:, ds(g * 6, 6)], half(o1, k3(m), h)).then_inc(o_stats, 1)

            with_late_update(NB - 1, lambda q: single_lo(0, 0, q, single=False), lambda q: single_lo(0, 1, q),
                        lambda q: single_lo(0, 2, q))
            with dve.Fori(3, NB) as i:
                for q in range(Q):
                    single_lo(0, i, q)
            dve.wait_ge(self_added, H * NB)

            def row_with_stats(m):
                single_lo(m, 0, 0)
                row_out3(m - 1)
                single_lo(m, 0, 1)
                single_lo(m, 0, 2)
                stats_o(m - 1)
                single_lo(m, 0, 3)

            row_with_stats(1)
            with dve.Fori(2, NB) as m:
                row_with_stats(m)
                with dve.Fori(1, m) as i:
                    for q in range(Q):
                        single_lo(m, i, q)
            row_out3(NB - 1)
            stats_o(NB - 1)

            fin = Chain(fin_step, 0)
            dve.wait_ge(o_stats, H * NB)
            V.bn_aggr(mv[:, :], ost).then_inc(fin_stats, 1)
            dve.wait_ge(fin_sum, 1)
            V.tensor_scalar_add(deg[:, 0:1], pD[:, 0:1], EPS_PN).then_inc(fin_var, 1)
            dve.wait_ge(fin_root, 1)
            fin(V.reciprocal(pn_scale, sq[:, 0:1]))
            newton(fin, pn_scale, deg[:, 0:1], deg[:, 3:4])
            fin(V.tensor_mul(pn_scale, pn_scale, deg[:, 3:4]))
            V.scalar_tensor_tensor(pn_bias, mv[:, 0:1], -1.0, pn_scale, ALU.mult, ALU.mult).then_inc(pn_ready, 1)

            def add_x1(k):
                for h in range(H):
                    dve.wait_ge(o_turned, k * H + (h + 1))
                    V.tensor_add(half(zr, k, h), (pA, pB)[h][:, :], half(ux, k, h)).then_inc(o_added, 1)
                for h in range(H):
                    dve.wait_ge(o_added, k * H + (h + 1))
                    for j in range(h * G, (h + 1) * G):
                        last = V.bn_stats(s1[:, ds(k * (BG * 6) + j * 6, 6)], zr[:, ds(k * BLK + j * P, P)])
                last.then_inc(sum_stats, 1)

            root = Chain(root_step, 0)
            for b in range(2):
                with dve.Fori(b * (BATCH + 1), (b + 1) * BATCH) as k:
                    add_x1(k)
                dve.wait_ge(sum_stats, (b + 1) * BATCH)
                at, size = b * BATCH * BG, BATCH * BG

                def place(first):
                    return s1[:, first + at:first + at + size]

                var = d[:, at:at + size]
                moments(root, s1[:, 6 * at:6 * (at + size)].rearrange("p (g t) -> p g t", t=6), place(MEAN), var,
                        place(TMP)).then_inc(fin_var, 1)
                if b == 0:
                    add_x1(BATCH)
                dve.wait_ge(fin_root, b + 2)
                root(V.reciprocal(place(RSTD), rsum[:, at:at + size]))
                newton(root, place(RSTD), var, place(TMP))
                root(V.tensor_mul(place(RSTD), place(RSTD), place(TMP)))
                V.scalar_tensor_tensor(place(BIAS), place(MEAN), -1.0, place(RSTD),
                                       ALU.mult, ALU.mult).then_inc(ln_ready, 1)
            dve.wait_ge(ln_ready, 2)
            with dve.Fori(NACT, NB) as k:
                for j in range(BG):
                    zg = zr[:, ds(k * BLK + j * P, P)]
                    last = V.tensor_scalar(zg, zg, s1[:, ds(k * BG + (j + RSTD), 1)],
                                           s1[:, ds(k * BG + (j + BIAS), 1)], ALU.mult, ALU.add)
                last.then_inc(dve_normed, 1)

        @block.tensor
        def _(pe):
            T = nc.tensor

            def multiply(n, o, q, layers, sums=None, single=True):
                for j in range(JB):
                    pe.wait_ge(slice_split, n + (o * JB + j + 1))
                    h_, l_ = hi[q % 2 * JB + j], lo[q % 2 * JB + j]
                    end = q == Q - 1 and j == JB - 1
                    for l, banks in layers:
                        p = q // 2 if single else l
                        for stat, moving in ((rhi[q % 2][p], (h_, l_)), (rlo[q % 2][p], (h_,))):
                            for h in range(H):
                                for mov in moving:
                                    last = T.matmul(banks[h][:, :], stat[:, j * P:j * P + P],
                                                    mov[:, h * HALF:(h + 1) * HALF], start=False,
                                                    stop=(end and stat is rlo[q % 2][p]), skip_group_check=True)
                    if sums and sums(q, j):
                        for h in range(H):
                            for mov in (h_, l_):
                                last = T.matmul(acc1[h][:, :], onesr[:, :], mov[:, h * HALF:(h + 1) * HALF],
                                                start=False, stop=(end and mov is l_), skip_group_check=True)
                    last.then_inc(slice_multiplied, 1)

            def open_banks(banks):
                for bank in banks:
                    T.matmul(bank[:, 0:2], ident[:, :], zero[:, 0:2], start=True, stop=False,
                             skip_group_check=True)

            def first_product(k, h):
                pe.wait_ge(xT_in, k * 16 + 16)
                for g in range(G):
                    at = h * HALF + g * P
                    last = T.matmul((pA, pB)[h][:, g * P:g * P + P], xT_blk[:, at:at + P], w0[:, :],
                                    start=True, stop=True)
                last.then_inc(y_done, 1)

            pe.wait_ge(consts_in, 64)
            pe.wait_ge(ones_set, 1)
            for h in range(H):
                first_product(0, h)

            def pair(k, i):
                for q in range(Q):
                    multiply(n1_pair(k, i), 2 * q, q, [(0, acc0)], sums=lambda q, j: True)

            def lower(k, i):
                for q in range(Q):
                    multiply(n1_rest(k, i), q, q, [(0, acc0)],
                             sums=lambda q, j: not summed_on_dve(q, j))

            def add_colsum():
                for h in range(H):
                    last = T.matmul(acc1[h][:, :], onesr[:, :].bitcast(f32), colsum[:, h * HALF:(h + 1) * HALF],
                                    start=False, stop=True, skip_group_check=True)
                last.then_inc(colsum_used, 1)

            def first_pair(k, start):
                if not start:
                    pe.wait_ge(acc0_read, k - 1)
                open_banks(acc0)
                if not start:
                    pe.wait_ge(banks_free, k - 1)
                open_banks(acc1)
                pair(k, 0)
                pe.wait_ge(z_ready, k)
                for h in range(H):
                    first_product(k, h)

            def row1(k, kind):
                phase1_blocks(pe, k, kind, lambda k: first_pair(k, kind == "first"), pair, None, lower,
                              add_colsum)

            pe.wait_ge(setup, 2)
            pe.wait_ge(ident_ready, 1)
            phase1_rows(pe, row1)

            def turn(src, dst):
                for j in range(G):
                    last = T.transpose(dst[:, j * P:j * P + P], src[:, j * P:j * P + P], ident[:, :])
                return last

            def turn_sum(m, h):
                g = m * H + h
                if h == 1:
                    pe.wait_ge(half_summed, m + 1)
                turn((t1, t2)[h], (pA, pB)[h]).then_inc(turned, 1)

            def turn_x1(m, h, first=False):
                g = m * H + h
                pe.wait_ge(x1_ready, g + 1)
                if not first:
                    pe.wait_ge(s1_ready, g)
                turn(t1, pC).then_inc(x1_turned, 1)

            def make_s1(m, h, first=False):
                g = m * H + h
                pe.wait_ge(x1T_ready, g + 1)
                if not first:
                    pe.wait_ge(self_added, g)
                for j in range(G):
                    T.matmul(pC[:, j * P:j * P + P], t2[:, j * P:j * P + P], w1[:, :], start=True, stop=True)
                T.matmul(pD[:, :], wsum[:, :], t2[:, :], start=True, stop=True).then_inc(s1_made, 1)

            def with_update(m, first, second, third, opens=None, start=False):
                first(0)
                turn_sum(m, 0)
                first(1)
                turn_sum(m, 1)
                first(2)
                first(3)
                if opens:
                    pe.wait_ge(*opens)
                    open_banks(acc1)
                second(0)
                second(1)
                turn_x1(m, 0, start)
                second(2)
                make_s1(m, 0, start)
                second(3)
                turn_x1(m, 1)
                third(0)
                make_s1(m, 1)
                third(1)
                third(2)
                third(3)
            def with_late_update(m, first, second, third, opens=None):
                first(0)
                turn_sum(m, 0)
                first(1)
                turn_sum(m, 1)
                first(2)
                first(3)
                if opens:
                    pe.wait_ge(*opens)
                    open_banks(acc1)
                second(0)
                second(1)
                second(2)
                turn_x1(m, 0)
                second(3)
                make_s1(m, 0)
                third(0)
                third(1)
                turn_x1(m, 1)
                third(2)
                make_s1(m, 1)
                third(3)

            L0, L1 = (0, acc0), (1, acc1)

            def diag(m, q):
                multiply(n2(m, 0), q, q, [L0], single=False)

            def dual(m, i, q):
                multiply(n2(m, i), q, q, [L0, L1], single=False)

            pe.wait_ge(acc0_read, NB - 1)
            open_banks(acc0)
            for q in range(Q):
                diag(0, q)
            pe.wait_ge(banks_free, row2(0))
            pe.wait_ge(acc0_read, NB)
            open_banks(acc0 + acc1)
            with_update(0, lambda q: diag(1, q), no_tile, lambda q: dual(1, 1, q), start=True)
            pe.wait_ge(banks_free, row2(1))
            pe.wait_ge(acc0_read, NB + 1)
            open_banks(acc0)
            with_update(1, lambda q: diag(2, q), lambda q: dual(2, 1, q), lambda q: dual(2, 2, q),
                        opens=(acc1_read, 1))
            with pe.Fori(3, NB) as m:
                pe.wait_ge(banks_free, row2(m - 1))
                pe.wait_ge(acc0_read, m + (NB - 1))
                open_banks(acc0)
                with_late_update(m - 1, lambda q: diag(m, q), lambda q: dual(m, 1, q), lambda q: dual(m, 2, q),
                            opens=(acc1_read, m - 1))
                with pe.Fori(3, m + 1) as i:
                    for q in range(Q):
                        dual(m, i, q)

            L3 = (1, acc0)

            def single(m, i, q, single=True):
                multiply(n3(m, i), q, q, [L3], single=single)

            pe.wait_ge(banks_free, row2(NB - 1))
            pe.wait_ge(acc0_read, 2 * NB - 1)
            open_banks(acc0)
            with_late_update(NB - 1, lambda q: single(0, 0, q, single=False), lambda q: single(0, 1, q),
                        lambda q: single(0, 2, q))
            with pe.Fori(3, NB) as i:
                for q in range(Q):
                    single(0, i, q)
            with pe.Fori(1, NB) as m:
                pe.wait_ge(banks_free, row3(m - 1))
                open_banks(acc0)
                with pe.Fori(0, m) as i:
                    for q in range(Q):
                        single(m, i, q)

            pe.wait_ge(fin_stats, 1)
            T.matmul(pD[:, 0:1], onesr[:, :].bitcast(f32), mv[:, 1:2], start=True, stop=True).then_inc(fin_sum, 1)

            def turn_o(k, h, first=False):
                pe.wait_ge(o_normed, k * H + (h + 1))
                if not first:
                    pe.wait_ge(o_added, k * H + (h - 1))
                turn((t1, t2)[h], (pA, pB)[h]).then_inc(o_turned, 1)

            for h in range(H):
                turn_o(0, h, first=True)
            with pe.Fori(1, NB) as k:
                for h in range(H):
                    turn_o(k, h)


def kernel(x, adj, L0_gnn_W, L0_gnn_b, L1_gnn_weight, L1_gnn_self_weight):
    import numpy as np
    import concourse.bacc as bacc
    from concourse.bass_utils import run_bass_kernel_spmd

    x, adj = np.asarray(x), np.asarray(adj)
    n, f = x.shape
    nb, q, jb = n // 1024, 4, 2
    blocks = adj.reshape(nb, 1024, nb, 1024)
    adj_t = np.ascontiguousarray(
        blocks.reshape(nb, 1024, nb, q, jb, 128).transpose(0, 2, 3, 5, 4, 1)).reshape(nb, nb, q, 128, jb * 1024)
    adj_n = np.ascontiguousarray(
        blocks.reshape(nb, q, jb, 128, nb, 1024).transpose(0, 4, 1, 3, 2, 5)).reshape(nb, nb, q, 128, jb * 1024)
    arrays = {
        "x": np.ascontiguousarray(x),
        "xT": np.ascontiguousarray(x.T),
        "adjT": adj_t,
        "adjN": adj_n,
        "W0": np.ascontiguousarray(L0_gnn_W),
        "b_rows": np.ascontiguousarray(np.broadcast_to(np.asarray(L0_gnn_b)[None, :], (128, f))),
        "W1": np.ascontiguousarray(L1_gnn_weight),
        "Wself": np.ascontiguousarray(L1_gnn_self_weight),
    }
    nc = bacc.Bacc("TRN2", target_bir_lowering=False, num_devices=1)
    f32 = mybir.dt.float32
    args = [nc.dram_tensor(f"in_{name}", a.shape, f32, kind="ExternalInput").ap() for name, a in arrays.items()]
    out = nc.dram_tensor("out", (n, f), f32, kind="ExternalOutput").ap()
    graph_kernel(nc, *args, out)
    r = run_bass_kernel_spmd(nc, [{f"in_{name}": a for name, a in arrays.items()}], core_ids=[0])
    return r.results[0]["out"]
```
